# Optimizing a Trainium2 kernel written in Bass

```python
import numpy as np
import jax
import jax.numpy as jnp

def _softmax(x, axis=-1):
    return jax.nn.softmax(x, axis=axis)

def _gelu(x):
    return jax.nn.gelu(x, approximate=True)

def _silu(x):
    return jax.nn.silu(x)

def _sigmoid(x):
    return jax.nn.sigmoid(x)

def _layernorm(x, axis=-1, eps=1e-05):
    m = jnp.mean(x, axis=axis, keepdims=True)
    v = jnp.var(x, axis=axis, keepdims=True)
    return (x - m) / jnp.sqrt(v + eps)

def _scatter_add(tgt, idx, src, axis=0):
    return tgt.at[idx].add(src)

def _segment_sum(src, seg, n):
    return jax.ops.segment_sum(src, seg, n)
kernel_name = 'mk_vit_tower_d1_tok_img1024_r4_061dac'

def setup_inputs(seed: int=0):
    np.random.seed(seed)
    _w = jnp.asarray

    def _rec_inputs():
        import jax
        import jax.numpy as jnp
        _rk = jax.random.key(seed)
        x = -0.00016672 + 0.999947 * jax.random.normal(jax.random.fold_in(_rk, 1), (32, 3, 96, 96), jnp.float32)
        return x
    x = _rec_inputs()

    def _L0_tok_setup():
        import jax, jax.numpy as jnp
        import numpy as np
        PATCH = 16

        def _patchify(x, p):
            B, C, H, W = x.shape
            nh, nw = (H // p, W // p)
            x = x.reshape(B, C, nh, p, nw, p)
            x = x.transpose(0, 2, 4, 1, 3, 5)
            return x.reshape(B, nh * nw, C * p * p)
        key = jax.random.key(seed)
        k1, k2, k3, k4, k5 = jax.random.split(key, 5)
        B, C, H = (64, 3, 96)
        d_model = 256
        p = PATCH
        num_patches = (H // p) ** 2
        in_dim = p * p * C
        x = jax.random.normal(k1, (B, C, H, H), dtype=jnp.float32)
        bound = 1.0 / np.sqrt(in_dim)
        W = jax.random.uniform(k2, (d_model, in_dim), dtype=jnp.float32, minval=-bound, maxval=bound)
        b = jax.random.uniform(k3, (d_model,), dtype=jnp.float32, minval=-bound, maxval=bound)
        cls_token = jax.random.normal(k4, (1, 1, d_model), dtype=jnp.float32)
        pos_enc = jax.random.normal(k5, (1, num_patches + 1, d_model), dtype=jnp.float32)
        return {'x': x, 'W': W, 'b': b, 'cls_token': cls_token, 'pos_enc': pos_enc}
    _L0_tok_all = _L0_tok_setup()
    _L0_tok_in = {k: v for k, v in _L0_tok_all.items() if k in ('W', 'b', 'cls_token', 'pos_enc')}
    del _L0_tok_all

    def _L0_attn_setup():
        import jax, jax.numpy as jnp
        import numpy as np
        D_MODEL = 256
        RANK = 64
        INIT_ALPHA = 0.5
        key = jax.random.key(seed)
        ks = jax.random.split(key, 12)
        D, R = (D_MODEL, RANK)
        s = 0.02
        return {'x': jax.random.normal(ks[0], (4, 512, D), dtype=jnp.float32), 'Wq': jax.random.normal(ks[1], (D, D), dtype=jnp.float32) * s, 'Wk': jax.random.normal(ks[2], (D, D), dtype=jnp.float32) * s, 'Wo': jax.random.normal(ks[3], (D, D), dtype=jnp.float32) * s, 'U_b': jax.random.normal(ks[4], (D, R), dtype=jnp.float32) * s, 'V_b': jax.random.normal(ks[5], (D, R), dtype=jnp.float32) * s, 'W_b': jax.random.normal(ks[6], (D, R), dtype=jnp.float32) * s, 'bias_b': jnp.zeros((D,), dtype=jnp.float32), 'U_t': jax.random.normal(ks[7], (D, R), dtype=jnp.float32) * s, 'V_t': jax.random.normal(ks[8], (D, R), dtype=jnp.float32) * s, 'W_t': jax.random.normal(ks[9], (D, R), dtype=jnp.float32) * s, 'X_t': jax.random.normal(ks[10], (D, R), dtype=jnp.float32) * s, 'bias_t': jnp.zeros((D,), dtype=jnp.float32), 'alpha': jnp.asarray(INIT_ALPHA, dtype=jnp.float32)}
    _L0_attn_all = _L0_attn_setup()
    _L0_attn_in = {k: v for k, v in _L0_attn_all.items() if k in ('Wq', 'Wk', 'Wo', 'U_b', 'V_b', 'W_b', 'bias_b', 'U_t', 'V_t', 'W_t', 'X_t', 'bias_t', 'alpha')}
    del _L0_attn_all

    def _L0_ffn_setup():
        import jax, jax.numpy as jnp
        import numpy as np
        B, T, D, F_FF, E, TOP_K = (8, 512, 256, 1024, 8, 2)
        CAP_FACTOR = 1.25
        key = jax.random.key(seed)
        ks = jax.random.split(key, 7)
        s = 0.02
        return {'x': jax.random.normal(ks[0], (B, T, D), dtype=jnp.float32), 'w_router': jax.random.normal(ks[1], (D, E), dtype=jnp.float32) * s, 'b_router': jnp.zeros((E,), dtype=jnp.float32), 'w1': jax.random.normal(ks[2], (E, D, F_FF), dtype=jnp.float32) * s, 'b1': jnp.zeros((E, F_FF), dtype=jnp.float32), 'w2': jax.random.normal(ks[3], (E, F_FF, D), dtype=jnp.float32) * s, 'b2': jnp.zeros((E, D), dtype=jnp.float32)}
    _L0_ffn_all = _L0_ffn_setup()
    _L0_ffn_in = {k: v for k, v in _L0_ffn_all.items() if k in ('w_router', 'b_router', 'w1', 'b1', 'w2', 'b2')}
    del _L0_ffn_all
    return {'x': x, 'L0_tok_W': _L0_tok_in['W'], 'L0_tok_b': _L0_tok_in['b'], 'L0_tok_cls_token': _L0_tok_in['cls_token'], 'L0_tok_pos_enc': _L0_tok_in['pos_enc'], 'L0_attn_Wq': _L0_attn_in['Wq'], 'L0_attn_Wk': _L0_attn_in['Wk'], 'L0_attn_Wo': _L0_attn_in['Wo'], 'L0_attn_U_b': _L0_attn_in['U_b'], 'L0_attn_V_b': _L0_attn_in['V_b'], 'L0_attn_W_b': _L0_attn_in['W_b'], 'L0_attn_bias_b': _L0_attn_in['bias_b'], 'L0_attn_U_t': _L0_attn_in['U_t'], 'L0_attn_V_t': _L0_attn_in['V_t'], 'L0_attn_W_t': _L0_attn_in['W_t'], 'L0_attn_X_t': _L0_attn_in['X_t'], 'L0_attn_bias_t': _L0_attn_in['bias_t'], 'L0_attn_alpha': _L0_attn_in['alpha'], 'L0_ffn_w_router': _L0_ffn_in['w_router'], 'L0_ffn_b_router': _L0_ffn_in['b_router'], 'L0_ffn_w1': _L0_ffn_in['w1'], 'L0_ffn_b1': _L0_ffn_in['b1'], 'L0_ffn_w2': _L0_ffn_in['w2'], 'L0_ffn_b2': _L0_ffn_in['b2']}

def reference(x, L0_tok_W, L0_tok_b, L0_tok_cls_token, L0_tok_pos_enc, L0_attn_Wq, L0_attn_Wk, L0_attn_Wo, L0_attn_U_b, L0_attn_V_b, L0_attn_W_b, L0_attn_bias_b, L0_attn_U_t, L0_attn_V_t, L0_attn_W_t, L0_attn_X_t, L0_attn_bias_t, L0_attn_alpha, L0_ffn_w_router, L0_ffn_b_router, L0_ffn_w1, L0_ffn_b1, L0_ffn_w2, L0_ffn_b2):
    import jax
    import jax.numpy as jnp

    def _L0_tok_ref(x, W, b, cls_token, pos_enc):
        import jax, jax.numpy as jnp
        import numpy as np
        PATCH = 16

        def _patchify(x, p):
            B, C, H, W = x.shape
            nh, nw = (H // p, W // p)
            x = x.reshape(B, C, nh, p, nw, p)
            x = x.transpose(0, 2, 4, 1, 3, 5)
            return x.reshape(B, nh * nw, C * p * p)
        B = x.shape[0]
        patches = _patchify(x, PATCH)
        proj = jnp.einsum('bnf,df->bnd', patches, W) + b
        cls = jnp.broadcast_to(cls_token, (B, 1, cls_token.shape[-1]))
        out = jnp.concatenate([cls, proj], axis=1) + pos_enc
        return out

    def _L0_attn_ref(x, Wq, Wk, Wo, U_b, V_b, W_b, bias_b, U_t, V_t, W_t, X_t, bias_t, alpha):
        import jax, jax.numpy as jnp
        import numpy as np
        D_MODEL = 256
        RANK = 64
        INIT_ALPHA = 0.5
        B, T, D = x.shape
        Q = x @ Wq.T
        K = x @ Wk.T
        counts = jnp.arange(1, T + 1, dtype=x.dtype)[None, :, None]
        Z = jnp.cumsum(x, axis=1) / counts
        a_b = Q @ V_b
        c_b = jnp.cumsum(K @ W_b, axis=1)
        bil = a_b * c_b @ U_b.T
        a_t = Q @ V_t
        c_t = jnp.cumsum(K @ W_t, axis=1)
        z_t = Z @ X_t
        tri = a_t * z_t * c_t @ U_t.T
        out = (bil + alpha * tri) / counts + (bias_b + alpha * bias_t)
        return out @ Wo.T

    def _L0_ffn_ref(x, w_router, b_router, w1, b1, w2, b2):
        import jax, jax.numpy as jnp
        import numpy as np
        B, T, D, F_FF, E, TOP_K = (8, 512, 256, 1024, 8, 2)
        CAP_FACTOR = 1.25
        b, t, d = x.shape
        n = b * t
        e = w_router.shape[1]
        xf = x.reshape(n, d)
        logits = xf.astype(jnp.float32) @ w_router + b_router
        gates = jax.nn.softmax(logits, axis=-1)
        topv, topi = jax.lax.top_k(gates, TOP_K)
        cap = max(1, int(CAP_FACTOR * n / e))
        e_flat = topi.reshape(-1)
        g_flat = topv.reshape(-1)
        tok = jnp.repeat(jnp.arange(n), TOP_K)
        onehot = jax.nn.one_hot(e_flat, e, dtype=jnp.int32)
        pos = jnp.cumsum(onehot, axis=0)[jnp.arange(n * TOP_K), e_flat] - 1
        keep = pos < cap
        posc = jnp.minimum(pos, cap - 1)
        buf = jnp.zeros((e, cap, d), x.dtype).at[e_flat, posc].add(jnp.where(keep[:, None], xf[tok], 0.0))
        h = jax.nn.gelu(jnp.einsum('ecd,edf->ecf', buf, w1) + b1[:, None, :], approximate=False)
        out = jnp.einsum('ecf,efd->ecd', h, w2) + b2[:, None, :]
        og = out[e_flat, posc]
        w = jnp.where(keep, g_flat, 0.0).astype(x.dtype)
        y = jnp.zeros((n, d), x.dtype).at[tok].add(w[:, None] * og)
        ws = jnp.zeros((n,), x.dtype).at[tok].add(w)
        y = jnp.where((ws > 0.0)[:, None], y / jnp.maximum(ws, 1e-06)[:, None], y)
        return y.reshape(b, t, d)
    h = _L0_tok_ref(x, L0_tok_W, L0_tok_b, L0_tok_cls_token, L0_tok_pos_enc)
    h = h + _L0_attn_ref(_layernorm(h, axis=-1), L0_attn_Wq, L0_attn_Wk, L0_attn_Wo, L0_attn_U_b, L0_attn_V_b, L0_attn_W_b, L0_attn_bias_b, L0_attn_U_t, L0_attn_V_t, L0_attn_W_t, L0_attn_X_t, L0_attn_bias_t, L0_attn_alpha)
    h = h + _L0_ffn_ref(_layernorm(h, axis=-1), L0_ffn_w_router, L0_ffn_b_router, L0_ffn_w1, L0_ffn_b1, L0_ffn_w2, L0_ffn_b2)
    return h

_drawn_inputs = setup_inputs


def setup_inputs(seed=0):
    import zlib

    import numpy as np

    out = dict(_drawn_inputs(seed))
    spreads = {'L0_attn_bias_b': (0.0, 0.8),
     'L0_attn_bias_t': (0.0, 2.0),
     'L0_ffn_b_router': (0.0, 0.587),
     'L0_ffn_b1': (0.0, 2.0),
     'L0_ffn_b2': (0.0, 0.8)}
    factors = {'L0_attn_Wq': 8.0,
     'L0_attn_Wk': 8.0,
     'L0_attn_U_b': 8.0,
     'L0_attn_V_b': 8.0,
     'L0_attn_W_b': 8.0,
     'L0_attn_U_t': 8.0,
     'L0_attn_V_t': 8.0,
     'L0_attn_W_t': 8.0,
     'L0_attn_X_t': 8.0,
     'L0_ffn_w_router': 3.625,
     'L0_ffn_w1': 5.353,
     'L0_ffn_w2': 3.592}
    for name, (base, spread) in spreads.items():
        noise = np.random.default_rng([zlib.crc32(name.encode()), seed]).standard_normal(out[name].shape)
        drawn = base * np.exp(spread * noise) if base else spread * noise
        out[name] = jnp.asarray(drawn.astype(out[name].dtype))
    for name, factor in factors.items():
        out[name] = (out[name] * factor).astype(out[name].dtype)
    return out
```

```python
import concourse.bass as bass
from concourse import mybir
from contextlib import ExitStack
import numpy as np

B, CH, IMG, PATCH = 32, 3, 96, 16
NP_ = IMG // PATCH
T = NP_ * NP_ + 1
N = B * T
D = 256
KD = D // 128
R = 64
NE, F = 8, 1024
KF = F // 128
CAP = max(1, int(1.25 * N / NE))
SLOT_TILES = 2
ST = -(-CAP // SLOT_TILES)
PAIRS = KF // 2
SL = ST * SLOT_TILES
TB = 3
TT = TB * T
NT = -(-N // TT)
LAST = N - (NT - 1) * TT
KP = CH * 2
IP = 96
IT = B * CH * NP_ // IP
ROW = D + NE
EPS = 1e-5
VECS = T + 4
GROUPS = [(0, 3), (3, 2), (5, 3), (8, 3)]
PROJ = [(0, 9), (9, 7), (16, 8), (24, 8)]

C_ID = 0
C_TRI = C_ID + 128
C_NEG = C_TRI + TT
C_IOTA = C_NEG + TT
C_IOTA8 = C_IOTA + SL
C_IDS = C_IOTA8 + NE
C_VALID = C_IDS + 3 * NT
C_RESET = C_VALID + NT
C_TRASH = C_RESET + NE * NT
C_LOW = C_TRASH + SLOT_TILES
C_EPS = C_LOW + 1
C_END = C_EPS + 1


def constants():
    c = np.zeros((128, C_END), np.float32)
    c[:, C_ID:C_ID + 128] = np.eye(128)
    m, n = np.arange(TT)[:, None], np.arange(TT)[None, :]
    c[:TT, C_TRI:C_TRI + TT] = np.where((m // T == n // T) & (m <= n), 1.0 / (n % T + 1), 0.0)
    c[:TT, C_NEG:C_NEG + TT] = np.where(m >= n, -1.0, 0.0)
    c[:, C_IOTA:C_IOTA + SL] = np.where(np.arange(SL) < CAP, np.arange(SL) + 1, -5)
    c[:, C_IOTA8:C_IOTA8 + NE] = np.arange(NE)
    p, t = np.arange(128)[:, None], np.arange(NT)[None, :]
    ids = c[:, C_IDS:C_IDS + 3 * NT].reshape(128, NT, 3)
    ids[:, :, 0], ids[:, :, 1], ids[:, :, 2] = p, t, 1.0
    c[:, C_VALID:C_VALID + NT] = (p < TT) & (t * TT + p < N)
    c[:, C_RESET:C_RESET + NE * NT] = np.arange(NE * NT) % NT != 0
    c[:, C_TRASH:C_TRASH + SLOT_TILES] = N + p + ST * np.arange(SLOT_TILES)[None, :]
    c[:, C_LOW] = np.arange(128) < R
    c[:, C_EPS] = EPS
    return c


def vit_block(nc, x, tok_w, tok_b, cls, pos, wq, wk, wo, u_b, v_b, w_b, bias_b,
              u_t, v_t, w_t, x_t, bias_t, alpha, w_router, b_router, w1, b1, w2, b2,
              const, xrows, out):
    f32, bf16, i32 = mybir.dt.float32, mybir.dt.bfloat16, mybir.dt.int32
    ALU, ACT, AX = mybir.AluOpType, mybir.ActivationFunctionType, mybir.AxisListType

    with ExitStack() as ctx:
        def sb(name, shape, dt=f32):
            return ctx.enter_context(nc.sbuf_tensor(name, shape, dt))

        def sem(name):
            return ctx.enter_context(nc.semaphore(name))

        cst = sb("cst", [128, C_END])
        ident = cst[:, C_ID:C_ID + 128]
        tri = cst[0:TT, C_TRI:C_TRI + TT]
        neg_prefix = cst[0:TT, C_NEG:C_NEG + TT]
        iota_slot = cst[0:TT, C_IOTA:C_IOTA + SL]
        iota_e = cst[0:TT, C_IOTA8:C_IOTA8 + NE]
        ids_f = cst[0:TT, C_IDS:C_IDS + 3 * NT]
        valid = cst[0:TT, C_VALID:C_VALID + NT]
        reset = cst[0:TT, C_RESET:C_RESET + NE * NT]
        trash = cst[0:ST, C_TRASH:C_TRASH + SLOT_TILES]
        eps_col = cst[:, C_EPS:C_EPS + 1]
        low_rows = cst[:, C_LOW:C_LOW + 1]

        ACOLS = IT * PATCH * IMG
        arena = sb("arena", [128, ACOLS])
        img = arena[0:IP, :].rearrange("p (a r w) -> p a r w", a=IT, r=PATCH)
        at = [0]

        def carve(rows, cols):
            at[0] += cols
            assert at[0] <= ACOLS
            return arena[0:rows, at[0] - cols:at[0]]

        onehot = [carve(TT, NT * SL // 2).bitcast(bf16).rearrange("p (t s) -> p t s", t=NT) for _ in range(2)]
        rows_in = [carve(ST, SLOT_TILES * ROW).rearrange("p (s c) -> p s c", s=SLOT_TILES) for _ in range(2)]
        buf_t = [carve(128, KD * SL).rearrange("p (k s) -> p k s", k=KD) for _ in range(2)]
        hid = carve(128, KF * SL).rearrange("p (k s) -> p k s", k=KF)
        out_t = carve(128, KD * SL).rearrange("p (k s) -> p k s", k=KD)
        out_s = [carve(ST, SLOT_TILES * D).rearrange("p (s c) -> p s c", s=SLOT_TILES) for _ in range(2)]

        patch_t = sb("patch_t", [128, KP, B * (T - 1)])
        h_t = sb("h_t", [128, KD, N])
        h2_t = sb("h2_t", [128, KD, N])
        xn_t = sb("xn_t", [128, KD, N])
        zx_t = sb("zx_t", [128, KD, N])
        z_s = sb("z_s", [128, N])
        prod = sb("prod", [128, N])
        xn = sb("xn", [TT, NT, D])
        h2 = sb("h2", [TT, NT, D])
        w1_s = [sb(f"w1_s{q}", [128, KD, F]) for q in range(2)]
        w2_s = [sb(f"w2_s{q}", [128, KF, D]) for q in range(2)]
        tok_w_s = sb("tok_w_s", [128, KD, KP * 128])
        tok_wt = sb("tok_wt", [128, KP, D])
        wq_s, wk_s, wo_s = (sb(n, [128, KD, D]) for n in ("wq_s", "wk_s", "wo_s"))
        wo_t = sb("wo_t", [128, KD, D])
        v_cat, w_cat, u_cat, xt_pad = (sb(n, [128, KD, 2 * R]) for n in ("v_cat", "w_cat", "u_cat", "xt_pad"))
        m_a = sb("m_a", [128, KD, 2 * R])
        m_c = sb("m_c", [128, KD, 2 * R])
        uw = sb("uw", [128, D])
        vec_rows = sb("vec_rows", [VECS, D])
        vec_t = sb("vec_t", [128, KD, VECS])
        b1_rows = sb("b1_rows", [NE * KF, 128])
        b2_rows = sb("b2_rows", [NE * KD, 128])
        b1_t = sb("b1_t", [128, NE * KF])
        b2_t = sb("b2_t", [128, NE * KD])
        alpha_s = sb("alpha_s", [128, 1])
        u_scale = sb("u_scale", [128, 1])
        bias_s = sb("bias_s", [128, KD])
        bias_o = sb("bias_o", [128, KD])
        table = sb("table", [128, KD, T])
        wr_s = sb("wr_s", [128, KD, NE])
        wr_c = sb("wr_c", [128, KD, NE])
        mean_mat = sb("mean_mat", [128, 128])
        ones = sb("ones", [TT, TT])
        zeros = sb("zeros", [ST, SLOT_TILES * D])
        b_router_s = sb("b_router_s", [TT, NE])
        ids = sb("ids", [TT, NT, 3], bf16)
        bn = sb("bn", [TT, 3, 6])
        mv = sb("mv", [TT, 2 * NT, 2])
        rstd = sb("rstd", [TT, 2 * NT])
        std = sb("std", [TT, 2 * NT])
        nmr = sb("nmr", [TT, 2 * NT])
        raw = sb("raw", [TT, NE, NT])
        route = [sb(f"route{n}", [TT, NE, NT]) for n in range(8)]
        so_far = sb("so_far", [TT, NE, NT])
        col = [sb(f"col{n}", [TT, NT]) for n in range(8)]
        dest = sb("dest", [TT, NE, NT])
        coef = sb("coef", [TT, NT, NE])
        info = sb("info", [ST, SLOT_TILES, 3])
        slot_a = sb("slot_a", [ST, SLOT_TILES])
        slot_b = sb("slot_b", [ST, SLOT_TILES])
        src_row = [sb(f"src_row{q}", [ST, SLOT_TILES], i32) for q in range(2)]
        b1_cur = [sb(f"b1_cur{q}", [128, KF]) for q in range(2)]
        b2_cur = [sb(f"b2_cur{q}", [128, KD]) for q in range(2)]
        coef_cur = [sb(f"coef_cur{q}", [ST, SLOT_TILES]) for q in range(2)]
        dst_row = [sb(f"dst_row{q}", [ST, SLOT_TILES], i32) for q in range(2)]

        ps = ctx.enter_context(nc.psum_tensor("ps", [128, 8 * 512], f32))

        def slot(u):
            return ps[:, (u % 4) * 1024:(u % 4 + 1) * 1024]

        def bank(b):
            return ps[:, b * 512:(b + 1) * 512]

        const_in, attn_in, vec_in, router_in, bias_in = (
            sem(n) for n in ("const_in", "attn_in", "vec_in", "router_in", "bias_in"))
        tok_w_in = sem("tok_w_in")
        img_in = [sem(f"img_in{n}") for n in range(IT)]
        pool_set = sem("pool_set")
        cut_dve, cut_pool, cut_act = sem("cut_dve"), sem("cut_pool"), sem("cut_act")
        psum_filled = sem("psum_filled")
        dve_drained = sem("dve_drained")
        act_drained = sem("act_drained")
        dve_step = sem("dve_step")
        var_ready, std_ready = sem("var_ready"), sem("std_ready")
        stats1_ready, stats2_ready = sem("stats1_ready"), sem("stats2_ready")
        rows_stored = [sem(f"rows_stored{g}") for g in range(len(GROUPS))]
        out_stored = sem("out_stored")
        added = sem("added")
        out_free = sem("out_free")
        coef_stored = sem("coef_stored")
        logits_ready, exp_ready = sem("logits_ready"), sem("exp_ready")
        chosen_ready, prefix_ready, coef_ready = sem("chosen_ready"), sem("prefix_ready"), sem("coef_ready")
        w1_in = [sem(f"w1_in{q}") for q in range(2)]
        w2_in = [sem(f"w2_in{q}") for q in range(2)]
        onehot_ready, info_ready, src_ready, dst_ready = (
            sem(n) for n in ("onehot_ready", "info_ready", "src_ready", "dst_ready"))
        gathered = [sem(f"gathered{q}") for q in range(2)]
        in_turned, buf_ready = sem("in_turned"), sem("buf_ready")
        up_done, hid_ready, down_done, out_t_ready = (
            sem(n) for n in ("up_done", "hid_ready", "down_done", "out_t_ready"))
        out_turned, out_s_ready = sem("out_turned"), sem("out_s_ready")
        find_step = sem("find_step")

        UNITS = [("tokw", 0, "act"), ("tokw", 1, "act"), ("vec", 0, "dve"), ("wo", 0, "act"),
                 ("mac", 0, "act"), ("uw", 0, "dve")]
        UNITS += [("img", k, "dve" if k % 2 else "act") for k in range(KP)]
        UNITS += [("proj", 0, "dve"), ("proj", 1, "dve"), ("norm1", 0, "act"), ("norm1", 1, "act")]
        UNITS += [("img", KP + k, "dve" if k % 2 else "act") for k in range(KP)]
        UNITS += [("xn_t", 0, "dve"), ("zx_t", 0, "act"), ("proj", 2, "dve"),
                  ("xn_t", 1, "dve"), ("zx_t", 1, "act"), ("proj", 3, "dve"),
                  ("norm1", 2, "act"), ("z", 0, "act"), ("ac", 0, "dve"),
                  ("norm1", 3, "act"), ("y", 0, "dve"), ("z", 1, "act"), ("ac", 1, "dve"),
                  ("xn_t", 2, "dve"), ("zx_t", 2, "act"), ("y", 1, "dve"),
                  ("norm2", 0, "act"), ("xn_t", 3, "dve"), ("zx_t", 3, "act"),
                  ("z", 2, "act"), ("ac", 2, "dve"), ("norm2", 1, "act"), ("y", 2, "dve"),
                  ("z", 3, "act"), ("ac", 3, "dve"), ("norm2", 2, "act"), ("y", 3, "dve"),
                  ("norm2", 3, "act"), ("prefix", 0, "dve")]
        PLACE = {(kind, n): u for u, (kind, n, _) in enumerate(UNITS)}

        def drained(eng, kind, n):
            u = PLACE[kind, n]
            reader = UNITS[u][2]
            eng.wait_ge(act_drained if reader == "act" else dve_drained,
                        sum(1 for v in UNITS[:u + 1] if v[2] == reader))

        def filled(eng, kind, n):
            eng.wait_ge(psum_filled, PLACE[kind, n] + 1)
            return slot(PLACE[kind, n])

        HALF = NP_ * 128
        staged = [buf[0:IP].rearrange("p k f -> p (k f)")[:, m * HALF:(m + 1) * HALF]
                  for buf in (w1_s[1], w2_s[1]) for m in range(2)]
        STAGERS = ("dve", "pool", "act")
        cut_by = {"dve": cut_dve, "pool": cut_pool, "act": cut_act}

        def cut(eng, name, copy, n):
            if n >= 2 * IT or STAGERS[n % 3] != name:
                return
            a, half = divmod(n, 2)
            eng.wait_ge(img_in[a], 16)
            if n >= 4:
                eng.wait_ge(psum_filled, PLACE["img", n - 4] + 1)
            copy(staged[n % 4].rearrange("p (j r q) -> p j r q", j=NP_, q=PATCH),
                 img[:, a, half * 8:half * 8 + 8].rearrange("p r (j q) -> p j r q", q=PATCH)).then_inc(cut_by[name], 1)

        def read_patches(copy, n, p):
            a, half = divmod(n, 2)
            pairs = IP // NP_
            src = p[:, 0:NP_ * 128].rearrange("p (j s) -> p j s", s=128)
            for c in range(CH):
                first = -(-(a * pairs - c) // CH)
                count = -(-((a + 1) * pairs - c) // CH) - first
                offset = (first * CH + c - a * pairs) * NP_
                dst = patch_t[:, 2 * c + half].rearrange("p (b i j) -> p j b i", i=NP_, j=NP_)
                of_c = src[:, :, offset:offset + count * CH * NP_].rearrange("p j (b c i) -> p j b c i", c=CH, i=NP_)[:, :, :, 0]
                ins = copy(dst[:, :, first:first + count], of_c)
            return ins

        def rows_of(t):
            return TT if t < NT - 1 else LAST

        def group_parts(g):
            t0, n = GROUPS[g]
            return [(TT, t0, t0 + n)] if t0 + n < NT else [(TT, t0, NT - 1), (LAST, NT - 1, NT)]

        def group_cols(g):
            t0, n = GROUPS[g]
            return t0 * TT, min(N, (t0 + n) * TT)

        block = ctx.enter_context(nc.Block())

        @block.sync
        def _(sp):
            sp.dma_start(cst[:, :], const).then_inc(const_in, 16)
            sp.dma_start(tok_w_s[:, :, :], tok_w.rearrange("(k p) f -> p k f", p=128)).then_inc(tok_w_in, 16)
            strips = x.rearrange("b c (i r) w -> (b c i) (r w)", r=PATCH)
            for a in range(IT):
                sp.dma_start(arena[0:IP, a * PATCH * IMG:(a + 1) * PATCH * IMG],
                             strips[a * IP:(a + 1) * IP]).then_inc(img_in[a], 16)
                if a == 1:
                    for w, dst in ((wq, wq_s), (wk, wk_s), (wo, wo_s)):
                        sp.dma_start(dst[:, :, :], w.rearrange("(k p) f -> p k f", p=128)).then_inc(attn_in, 16)

            def load_w1(e, q):
                sp.dma_start(w1_s[q][:, :, :], w1[e].rearrange("(k p) f -> p k f", p=128)).then_inc(w1_in[q], 16)

            def load_w2(e, q):
                sp.dma_start(w2_s[q][:, :, :], w2[e].rearrange("(k p) d -> p k d", p=128)).then_inc(w2_in[q], 16)

            load_w1(0, 0)
            load_w2(0, 0)
            sp.wait_ge(psum_filled, PLACE["img", 2 * IT - 1] + 1)
            load_w1(1, 1)
            load_w2(1, 1)
            sp.wait_ge(pool_set, 5)
            sp.dma_start(out[N:N + SL].rearrange("(p s) d -> p (s d)", p=ST), zeros[:, :]).then_inc(out_stored, 16)

            def tile_rows(dram, lo, hi, t0, n):
                return dram[t0 * TT:(t0 + n) * TT, lo:hi].rearrange("(t p) d -> p t d", p=TT)

            for g, (t0, n) in enumerate(GROUPS):
                whole = n - (t0 + n == NT)
                drained(sp, "norm2", g)
                sp.dma_start(tile_rows(xrows, 0, D, t0, whole), xn[:, t0:t0 + whole]).then_inc(rows_stored[g], 16)
                sp.dma_start(tile_rows(out, 0, D, t0, whole), h2[:, t0:t0 + whole]).then_inc(out_stored, 16)
                if whole < n:
                    sp.dma_start(xrows[N - LAST:N, 0:D], xn[0:LAST, NT - 1]).then_inc(rows_stored[g], 16)
                    sp.dma_start(out[N - LAST:N], h2[0:LAST, NT - 1]).then_inc(out_stored, 16)
            sp.wait_ge(coef_ready, 1)
            sp.dma_start(tile_rows(xrows, D, ROW, 0, NT - 1), coef[:, 0:NT - 1]).then_inc(coef_stored, 16)
            sp.dma_start(xrows[N - LAST:N, D:ROW], coef[0:LAST, NT - 1]).then_inc(coef_stored, 16)
            with sp.Fori(0, NE // 2 - 1) as i:
                for q in range(2):
                    e = 2 * i + q + 2
                    sp.wait_ge(up_done, (e - 1) * PAIRS)
                    load_w1(e, q)
                    sp.wait_ge(down_done, e - 1)
                    load_w2(e, q)

        @block.gpsimd
        def _(pool):
            pool.memset(xt_pad[:, :, 0:R], 0.0).then_inc(pool_set, 1)
            pool.memset(mean_mat[:, :], 1.0 / D).then_inc(pool_set, 1)
            pool.memset(ones[:, :], 1.0).then_inc(pool_set, 1)
            pool.memset(u_scale[:, :], 1.0).then_inc(pool_set, 1)
            pool.memset(zeros[:, :], 0.0).then_inc(pool_set, 1)
            pool.memset(raw[:, :, :], 0.0).then_inc(pool_set, 1)
            pool.memset(rstd[:, :], 1.0).then_inc(pool_set, 1)
            pool.memset(coef[:, :, :], 0.0).then_inc(pool_set, 1)
            for n in range(2 * IT):
                cut(pool, "pool", pool.tensor_copy, n)

            def gather(e, q):
                pool.wait_ge(src_ready, e + 1)
                for s in range(SLOT_TILES):
                    pool.indirect_dma_start(
                        out=rows_in[q][:, s, :], out_offset=None, in_=xrows[:, :],
                        in_offset=bass.IndirectOffsetOnAxis(ap=src_row[q][:, s:s + 1], axis=0),
                    ).then_inc(gathered[q], 16)

            def add_out(e, q):
                if e == 0:
                    pool.wait_ge(out_stored, 16 * (len(GROUPS) + 2))
                else:
                    pool.wait_ge(added, e * 16 * SLOT_TILES)
                pool.sem_inc(out_free, 1)
                pool.wait_ge(dst_ready, e + 1)
                pool.wait_ge(out_s_ready, e + 1)
                for s in range(SLOT_TILES):
                    pool.indirect_dma_start(
                        out=out[:, :], out_offset=bass.IndirectOffsetOnAxis(ap=dst_row[q][:, s:s + 1], axis=0),
                        in_=out_s[q][:, s, :], in_offset=None, compute_op=ALU.add,
                    ).then_inc(added, 16)

            for g, (t0, n) in enumerate(GROUPS):
                pool.wait_ge(rows_stored[g], 16 * (1 + (t0 + n == NT)))
            pool.wait_ge(coef_stored, 32)
            gather(0, 0)
            for e in range(NE):
                if e > 0:
                    add_out(e - 1, (e - 1) % 2)
                if e < NE - 1:
                    gather(e + 1, (e + 1) % 2)
            add_out(NE - 1, (NE - 1) % 2)
            pool.wait_ge(added, NE * 16 * SLOT_TILES)

        @block.scalar
        def _(act):
            for r0, src in ((0, pos[0]), (T, cls[0]), (T + 1, tok_b), (T + 2, bias_b), (T + 3, bias_t)):
                src = src if len(src.shape) == 2 else src.rearrange("(a n) -> a n", a=1)
                n = src.shape[0]
                act.dma_start(vec_rows[r0:r0 + n, :], src).then_inc(vec_in, 16)
            for src, dst in ((v_b, v_cat[:, :, 0:R]), (v_t, v_cat[:, :, R:]), (w_b, w_cat[:, :, 0:R]),
                             (w_t, w_cat[:, :, R:]), (u_b, u_cat[:, :, 0:R]), (u_t, u_cat[:, :, R:]),
                             (x_t, xt_pad[:, :, R:])):
                act.dma_start(dst, src.rearrange("(k p) r -> p k r", p=128)).then_inc(attn_in, 16)
            act.dma_start(alpha_s[:, :], alpha.rearrange("(a n) -> a n", a=1).broadcast_to((128, 1))).then_inc(attn_in, 16)
            act.dma_start(wr_s[:, :, :], w_router.rearrange("(k p) e -> p k e", p=128)).then_inc(router_in, 16)
            act.dma_start(b_router_s[:, :], b_router.rearrange("(a n) -> a n", a=1).broadcast_to((TT, NE))).then_inc(router_in, 16)
            act.dma_start(b1_rows[:, :], b1.rearrange("e (k p) -> (e k) p", p=128)).then_inc(bias_in, 16)
            act.dma_start(b2_rows[:, :], b2.rearrange("e (k p) -> (e k) p", p=128)).then_inc(bias_in, 16)

            def copy(dst, src):
                return act.activation(dst, src, ACT.Copy)

            stds = [0]

            def take_roots(g, base):
                stds[0] += 1
                act.wait_ge(var_ready, stds[0])
                for r, a, b in group_parts(g):
                    ins = act.activation(std[0:r, base + a:base + b], mv[0:r, base + a:base + b, 1], ACT.Sqrt,
                                         bias=eps_col[0:r])
                ins.then_inc(std_ready, 1)

            def norm1(g):
                take_roots(g, 0)
                act.wait_ge(stats1_ready, g + 1)
                p = slot(PLACE["norm1", g])
                t0, n = GROUPS[g]
                for i in range(n):
                    t = t0 + i
                    r = rows_of(t)
                    ins = act.activation(xn[0:r, t], p[0:r, i * D:(i + 1) * D], ACT.Identity,
                                         bias=nmr[0:r, t:t + 1], scale=rstd[0:r, t:t + 1])
                ins.then_inc(act_drained, 1)

            def norm2(g):
                take_roots(g, NT)
                act.wait_ge(stats2_ready, g + 1)
                drained(act, "xn_t", g)
                p = slot(PLACE["norm2", g])
                t0, n = GROUPS[g]
                for i in range(n):
                    t = t0 + i
                    r = rows_of(t)
                    act.activation(xn[0:r, t], p[0:r, i * D:(i + 1) * D], ACT.Identity,
                                   bias=nmr[0:r, NT + t:NT + t + 1], scale=rstd[0:r, NT + t:NT + t + 1])
                whole = n - (t0 + n == NT)
                ins = copy(h2[:, t0:t0 + whole], p[0:TT, 0:whole * D].rearrange("p (t d) -> p t d", t=whole))
                if whole < n:
                    ins = copy(h2[0:LAST, NT - 1], p[0:LAST, whole * D:n * D])
                ins.then_inc(act_drained, 1)

            for kind, n, reader in UNITS:
                if (kind, n) == ("mac", 0):
                    for m in range(4):
                        cut(act, "act", copy, m)
                if kind == "img" and reader != "act":
                    cut(act, "act", copy, n + 4)
                if reader != "act":
                    continue
                if kind == "tokw":
                    p = filled(act, kind, n)
                    copy(tok_wt[:, 3 * n:3 * n + 3], p[:, 0:3 * D].rearrange("p (k d) -> p k d", k=3)).then_inc(act_drained, 1)
                elif kind == "wo":
                    p = filled(act, kind, n)
                    copy(wo_t[:, :, :], p[:, 0:KD * D].rearrange("p (k d) -> p k d", k=KD)).then_inc(act_drained, 1)
                elif kind == "mac":
                    p = filled(act, kind, n)
                    copy(m_a[:, :, :], p[:, 0:256].rearrange("p (k r) -> p k r", k=KD))
                    copy(m_c[:, :, :], p[:, 256:512].rearrange("p (k r) -> p k r", k=KD)).then_inc(act_drained, 1)
                elif kind == "img":
                    read_patches(copy, n, filled(act, kind, n)).then_inc(act_drained, 1)
                    cut(act, "act", copy, n + 4)
                elif kind == "norm1":
                    norm1(n)
                elif kind == "zx_t":
                    c0, c1 = group_cols(n)
                    p = filled(act, kind, n).rearrange("p (k s) -> p k s", k=KD)
                    copy(zx_t[:, :, c0:c1], p[:, :, 0:c1 - c0]).then_inc(act_drained, 1)
                elif kind == "z":
                    c0, c1 = group_cols(n)
                    p = filled(act, kind, n)
                    act.activation(z_s[:, c0:c1], p[:, 0:c1 - c0], ACT.Identity, bias=low_rows).then_inc(act_drained, 1)
                elif kind == "norm2":
                    norm2(n)
            act.wait_ge(logits_ready, 1)
            act.activation(route[1][:, :, :], route[0][:, :, :], ACT.Exp).then_inc(exp_ready, 1)

            def hidden(e, q, pair):
                act.wait_ge(up_done, e * PAIRS + pair + 1)
                for f in (2 * pair, 2 * pair + 1):
                    ins = act.activation(hid[:, f, :], bank(pair)[:, (f % 2) * SL:(f % 2 + 1) * SL], ACT.Gelu,
                                         bias=b1_cur[q][:, f:f + 1])
                ins.then_inc(hid_ready, 1)

            def weigh(e, q):
                act.wait_ge(out_turned, e + 1)
                act.wait_ge(out_free, e + 1)
                for s in range(SLOT_TILES):
                    ins = act.activation(out_s[q][:, s, :], bank(6)[0:ST, s * D:(s + 1) * D], ACT.Copy,
                                         scale=coef_cur[q][:, s:s + 1])
                ins.then_inc(out_s_ready, 1)

            for pair in range(PAIRS):
                hidden(0, 0, pair)
            with act.Fori(0, NE // 2 - 1) as i:
                for j in range(2):
                    e = 2 * i + 1 + j
                    hidden(e, 1 - j, 0)
                    weigh(e - 1, j)
                    for pair in range(1, PAIRS):
                        hidden(e, 1 - j, pair)
            hidden(NE - 1, 1, 0)
            weigh(NE - 2, 0)
            for pair in range(1, PAIRS):
                hidden(NE - 1, 1, pair)
            weigh(NE - 1, 1)

        @block.vector
        def _(dve):
            steps, stds = [0], [0]

            def step(ins):
                steps[0] += 1
                ins.then_inc(dve_step, 1)
                dve.wait_ge(dve_step, steps[0])

            def stats(p, g, base, ready):
                t0, n = GROUPS[g]
                for i in range(n):
                    r = rows_of(t0 + i)
                    ins = dve.bn_stats(bn[0:r, i], p[0:r, i * D:(i + 1) * D])
                step(ins)
                for i in range(n):
                    r = rows_of(t0 + i)
                    ins = dve.bn_aggr(mv[0:r, base + t0 + i], bn[0:r, i])
                ins.then_inc(var_ready, 1)
                stds[0] += 1
                parts = group_parts(g)
                dve.wait_ge(std_ready, stds[0])
                for r, a, b in parts:
                    ins = dve.reciprocal(rstd[0:r, base + a:base + b], std[0:r, base + a:base + b])
                step(ins)
                for r, a, b in parts:
                    ins = dve.scalar_tensor_tensor(nmr[0:r, base + a:base + b], mv[0:r, base + a:base + b, 0], -1.0,
                                                   rstd[0:r, base + a:base + b], ALU.mult, ALU.mult)
                ins.then_inc(ready, 1)

            dve.wait_ge(const_in, 16)
            dve.tensor_copy(ids[:, :, :], ids_f.rearrange("p (t c) -> p t c", c=3))
            dve.wait_ge(pool_set, 8)
            dve.wait_ge(attn_in, 16 * 11)
            step(dve.tensor_copy(u_scale[R:, :], alpha_s[R:, :]))

            for kind, n, reader in UNITS:
                if (kind, n) == ("mac", 0):
                    for m in range(4):
                        cut(dve, "dve", dve.tensor_copy, m)
                if kind == "img" and reader != "dve":
                    cut(dve, "dve", dve.tensor_copy, n + 4)
                if kind == "norm1":
                    stats(filled(dve, kind, n), n, 0, stats1_ready)
                    continue
                if kind == "norm2":
                    p = filled(dve, kind, n)
                    t0, c = GROUPS[n]
                    for i in range(c):
                        r = rows_of(t0 + i)
                        dve.tensor_copy(raw[0:r, :, t0 + i], p[0:r, 3 * D + i * NE:3 * D + (i + 1) * NE])
                    stats(p, n, NT, stats2_ready)
                    continue
                if reader != "dve":
                    continue
                if kind == "vec":
                    p = filled(dve, kind, n)
                    dve.tensor_copy(b1_t[:, :], p[:, 128:128 + NE * KF])
                    dve.tensor_copy(b2_t[:, :], p[:, 192:192 + NE * KD])
                    step(dve.tensor_copy(vec_t[:, :, :], p[:, 0:KD * VECS].rearrange("p (k v) -> p k v", k=KD)))
                    for k in range(KD):
                        dve.tensor_scalar(table[:, k, 1:T], vec_t[:, k, 1:T], vec_t[:, k, T + 1:T + 2], None, ALU.add)
                    dve.tensor_tensor(table[:, :, 0:1], vec_t[:, :, 0:1], vec_t[:, :, T:T + 1], ALU.add)
                    step(dve.scalar_tensor_tensor(bias_s[:, :], vec_t[:, :, T + 3], alpha_s[:, :], vec_t[:, :, T + 2],
                                                  ALU.mult, ALU.add))
                    dve.tensor_copy(h_t[:, :, :].rearrange("p k (b t) -> p k b t", t=T)[:, :, :, 0],
                                    table[:, :, 0:1].broadcast_to((128, KD, B))).then_inc(dve_drained, 1)
                elif kind == "uw":
                    p = filled(dve, kind, n)
                    dve.tensor_scalar(uw[:, :], p[:, 0:D], u_scale[:, 0:1], None, ALU.mult)
                    dve.wait_ge(router_in, 32)
                    for k in range(KD):
                        dve.tensor_tensor(wr_c[:, k], wr_s[:, k], p[:, 264:264 + NE], ALU.subtract)
                    dve.tensor_copy(bias_o[:, :], p[:, 256:256 + KD]).then_inc(dve_drained, 1)
                elif kind == "img":
                    read_patches(dve.tensor_copy, n, filled(dve, kind, n)).then_inc(dve_drained, 1)
                    cut(dve, "dve", dve.tensor_copy, n + 4)
                elif kind == "proj":
                    p = filled(dve, kind, n)
                    b0, nb = PROJ[n]
                    for k in range(KD):
                        dst = h_t[:, k, b0 * T:(b0 + nb) * T].rearrange("p (b t) -> p b t", t=T)[:, :, 1:T]
                        src = p[:, k * 512:k * 512 + nb * (T - 1)].rearrange("p (b t) -> p b t", t=T - 1)
                        ins = dve.tensor_tensor(dst, src, table[:, k:k + 1, 1:T].broadcast_to((128, nb, T - 1)), ALU.add)
                    ins.then_inc(dve_drained, 1)
                elif kind == "xn_t":
                    c0, c1 = group_cols(n)
                    p = filled(dve, kind, n).rearrange("p (k s) -> p k s", k=KD)
                    dve.tensor_copy(xn_t[:, :, c0:c1], p[:, :, 0:c1 - c0]).then_inc(dve_drained, 1)
                elif kind == "ac":
                    c0, c1 = group_cols(n)
                    p = filled(dve, kind, n)
                    drained(dve, "z", n)
                    step(dve.tensor_tensor(z_s[:, c0:c1], p[:, 512:512 + c1 - c0], z_s[:, c0:c1], ALU.mult))
                    dve.tensor_tensor(prod[:, c0:c1], p[:, 0:c1 - c0], z_s[:, c0:c1], ALU.mult).then_inc(dve_drained, 1)
                elif kind == "y":
                    c0, c1 = group_cols(n)
                    p = filled(dve, kind, n)
                    for k in range(KD):
                        ins = dve.scalar_tensor_tensor(h2_t[:, k, c0:c1], p[:, k * 512:k * 512 + c1 - c0], bias_o[:, k:k + 1],
                                                       h_t[:, k, c0:c1], ALU.add, ALU.add)
                    ins.then_inc(dve_drained, 1)
                elif kind == "prefix":
                    lg, ex, g, eq, key, o1, o2, both = (r[:, :, :] for r in route)
                    mx, sm, rs, i1, m2, i2, ws, rw = (c[:, :] for c in col)

                    def per_token(c):
                        return c.rearrange("p (a t) -> p a t", a=1).broadcast_to((TT, NE, NT))

                    def per_expert(c):
                        return c.rearrange("p (e a) -> p e a", a=1).broadcast_to((TT, NE, NT))

                    def over_experts(r):
                        return r.rearrange("p e t -> p t e")

                    step(dve.tensor_tensor(lg, raw[:, :, :], per_token(rstd[:, NT:]), ALU.mult))
                    step(dve.tensor_tensor(lg, lg, per_expert(b_router_s[:, :]), ALU.add))
                    step(dve.tensor_reduce(mx, over_experts(lg), AX.X, ALU.max))
                    dve.tensor_tensor(lg, lg, per_token(mx), ALU.subtract).then_inc(logits_ready, 1)
                    dve.wait_ge(exp_ready, 1)
                    step(dve.tensor_reduce(sm, over_experts(ex), AX.X, ALU.add))
                    step(dve.reciprocal(rs, sm))
                    step(dve.tensor_tensor(g, ex, per_token(rs), ALU.mult))

                    def choose(vals, best, first, mask):
                        step(dve.tensor_reduce(best, over_experts(vals), AX.X, ALU.max))
                        step(dve.tensor_tensor(eq, vals, per_token(best), ALU.is_equal))
                        step(dve.scalar_tensor_tensor(key, eq, -float(NE), per_expert(iota_e), ALU.mult, ALU.add))
                        step(dve.tensor_reduce(first, over_experts(key), AX.X, ALU.min))
                        step(dve.tensor_scalar(first, first, float(NE), None, ALU.add))
                        step(dve.tensor_tensor(mask, per_expert(iota_e), per_token(first), ALU.is_equal))

                    choose(g, m2, i1, o1)
                    step(dve.scalar_tensor_tensor(lg, o1, -2.0, g, ALU.mult, ALU.add))
                    choose(lg, m2, i2, o2)
                    step(dve.tensor_tensor(both, o1, o2, ALU.add))
                    step(dve.tensor_tensor(both, both, per_token(valid), ALU.mult))
                    dve.tensor_tensor_scan(so_far[:, :, :].rearrange("p e t -> p (e t)"), reset,
                                           both.rearrange("p e t -> p (e t)"), 0.0, ALU.mult, ALU.add).then_inc(chosen_ready, 1)

                    p = filled(dve, kind, n)
                    before = p[0:TT, 0:NE * NT].rearrange("p (e t) -> p e t", e=NE)
                    dve.scalar_tensor_tensor(dest[:, :, :], before, 1.0, both, ALU.add, ALU.mult)
                    step(dve.scalar_tensor_tensor(key, before, float(CAP), both, ALU.is_lt, ALU.mult))
                    step(dve.tensor_tensor(key, key, g, ALU.mult))
                    step(dve.tensor_reduce(ws, over_experts(key), AX.X, ALU.add))
                    step(dve.tensor_scalar(ws, ws, 1e-6, None, ALU.max))
                    step(dve.reciprocal(rw, ws))
                    dve.tensor_tensor(coef[:, :, :], over_experts(key),
                                      rw.rearrange("p (t a) -> p t a", a=1).broadcast_to((TT, NT, NE)),
                                      ALU.mult).then_inc(coef_ready, 1)

            def find(e, q):
                place = dest[:, bass.ds(e, 1), :].rearrange("p a t -> p t a").broadcast_to((TT, NT, SL))
                dve.tensor_tensor(onehot[q], iota_slot.rearrange("p (a s) -> p a s", a=1).broadcast_to((TT, NT, SL)),
                                  place, ALU.is_equal).then_inc(onehot_ready, 1)

            def rows(e, q, before):
                dve.wait_ge(info_ready, e + 1)
                dve.tensor_copy(info[:, :, :], bank(5)[0:ST, 400:400 + 3 * SLOT_TILES].rearrange("p (s c) -> p s c", c=3)
                                ).then_inc(find_step, 1)
                dve.wait_ge(find_step, 2 * e + 1)
                dve.scalar_tensor_tensor(src_row[q][:, :], info[:, :, 1], float(TT), info[:, :, 0],
                                         ALU.mult, ALU.add).then_inc(src_ready, 1)
                dve.scalar_tensor_tensor(slot_a[:, :], info[:, :, 1], float(TT), info[:, :, 0], ALU.mult, ALU.add)
                dve.scalar_tensor_tensor(slot_b[:, :], info[:, :, 2], 0.0, trash, ALU.is_equal, ALU.mult
                                         ).then_inc(find_step, 1)
                dve.wait_ge(find_step, 2 * e + 2)
                if before:
                    dve.wait_ge(added, (e - 1) * 16 * SLOT_TILES)
                dve.tensor_tensor(dst_row[q][:, :], slot_a[:, :], slot_b[:, :], ALU.add).then_inc(dst_ready, 1)

            def take_in(e, q, before):
                dve.wait_ge(in_turned, e + 1)
                if before:
                    dve.wait_ge(out_s_ready, e - 1)
                dve.tensor_copy(coef_cur[q][:, :], rows_in[q][:, :, bass.ds(D + e, 1)])
                dve.tensor_copy(b1_cur[q][:, :], b1_t[:, bass.ds(e * KF, KF)])
                dve.tensor_copy(b2_cur[q][:, :], b2_t[:, bass.ds(e * KD, KD)])
                dve.tensor_copy(buf_t[q], bank(5)[:, 0:KD * SL].rearrange("p (k s) -> p k s", k=KD)).then_inc(buf_ready, 1)

            def read_out(e, q):
                dve.wait_ge(down_done, e + 1)
                for k in range(KD):
                    ins = dve.tensor_scalar(out_t[:, k, :], bank(4)[:, k * SL:(k + 1) * SL], b2_cur[q][:, k:k + 1],
                                            None, ALU.add)
                ins.then_inc(out_t_ready, 1)

            find(0, 0)
            rows(0, 0, False)
            take_in(0, 0, False)
            find(1, 1)
            rows(1, 1, False)
            take_in(1, 1, False)
            read_out(0, 0)
            with dve.Fori(0, NE // 2 - 1) as i:
                for j in range(2):
                    e = 2 * i + 1 + j
                    find(e + 1, j)
                    rows(e + 1, j, True)
                    take_in(e + 1, j, True)
                    read_out(e, 1 - j)
            read_out(NE - 1, 1)

        @block.tensor
        def _(pe):
            def claim(u):
                if u >= 4:
                    drained(pe, *UNITS[u - 4][:2])

            for u, (kind, n, _reader) in enumerate(UNITS):
                claim(u)
                p = slot(u)
                if kind == "tokw":
                    pe.wait_ge(const_in, 16)
                    pe.wait_ge(tok_w_in, 16)
                    for k in range(3 * n, 3 * n + 3):
                        for d in range(KD):
                            o = (k - 3 * n) * D + d * 128
                            ins = pe.transpose(p[:, o:o + 128], tok_w_s[:, d, k * 128:(k + 1) * 128], ident)
                elif kind == "vec":
                    pe.wait_ge(vec_in, 80)
                    pe.wait_ge(bias_in, 32)
                    for k in range(KD):
                        pe.transpose(p[:, k * VECS:(k + 1) * VECS], vec_rows[:, k * 128:(k + 1) * 128], ident[0:VECS, 0:VECS])
                    pe.transpose(p[:, 128:128 + NE * KF], b1_rows[:, :], ident[0:NE * KF, 0:NE * KF])
                    ins = pe.transpose(p[:, 192:192 + NE * KD], b2_rows[:, :], ident[0:NE * KD, 0:NE * KD])
                elif kind == "wo":
                    pe.wait_ge(attn_in, 16 * 11)
                    for d in range(KD):
                        for k in range(KD):
                            o = d * D + k * 128
                            ins = pe.transpose(p[:, o:o + 128], wo_s[:, k, d * 128:(d + 1) * 128], ident)
                elif kind == "mac":
                    pe.wait_ge(pool_set, 1)
                    for m, (w, v) in enumerate(((wq_s, v_cat), (wk_s, w_cat))):
                        for d in range(KD):
                            for k in range(KD):
                                o = m * 256 + d * 128
                                ins = pe.matmul(p[:, o:o + 128], w[:, k, d * 128:(d + 1) * 128], v[:, k, :],
                                                start=k == 0, stop=k == KD - 1)
                elif kind == "uw":
                    drained(pe, "vec", 0)
                    drained(pe, "wo", 0)
                    pe.wait_ge(router_in, 32)
                    pe.wait_ge(pool_set, 2)
                    for k in range(KD):
                        pe.matmul(p[:, 0:D], u_cat[:, k, :], wo_t[:, k, :], start=k == 0, stop=k == KD - 1)
                    for o in range(KD):
                        for k in range(KD):
                            pe.matmul(p[:, 256 + o:257 + o], wo_t[:, k, o * 128:(o + 1) * 128], bias_s[:, k:k + 1],
                                      start=k == 0, stop=k == KD - 1)
                    for k in range(KD):
                        ins = pe.matmul(p[:, 264:264 + NE], mean_mat[:, :], wr_s[:, k, :], start=k == 0, stop=k == KD - 1)
                elif kind == "img":
                    pe.wait_ge(cut_by[STAGERS[n % 3]], n // 3 + 1)
                    for j in range(NP_):
                        ins = pe.transpose(p[:, j * 128:j * 128 + IP], staged[n % 4][:, j * 128:(j + 1) * 128],
                                           ident[0:IP, 0:IP])
                elif kind == "proj":
                    b0, nb = PROJ[n]
                    a = ((b0 + nb) * CH * NP_ - 1) // IP
                    drained(pe, "img", 2 * a)
                    drained(pe, "img", 2 * a + 1)
                    drained(pe, "tokw", 1)
                    for d in range(KD):
                        for k in range(KP):
                            ins = pe.matmul(p[:, d * 512:d * 512 + nb * 36], tok_wt[:, k, d * 128:(d + 1) * 128],
                                            patch_t[:, k, b0 * 36:(b0 + nb) * 36], start=k == 0, stop=k == KP - 1)
                elif kind in ("norm1", "norm2"):
                    src = h_t if kind == "norm1" else h2_t
                    if kind == "norm1":
                        drained(pe, "proj", n)
                    else:
                        drained(pe, "y", n)
                    t0, c = GROUPS[n]
                    for i in range(c):
                        r = rows_of(t0 + i)
                        cols = slice((t0 + i) * TT, (t0 + i) * TT + r)
                        for k in range(KD):
                            ins = pe.transpose(p[0:r, i * D + k * 128:i * D + (k + 1) * 128], src[:, k, cols], ident)
                        if kind == "norm2":
                            for k in range(KD):
                                ins = pe.matmul(p[0:r, 3 * D + i * NE:3 * D + (i + 1) * NE], src[:, k, cols], wr_c[:, k, :],
                                                start=k == 0, stop=k == KD - 1)
                elif kind in ("xn_t", "zx_t"):
                    drained(pe, "norm1", n)
                    t0, c = GROUPS[n]
                    for i in range(c):
                        r = rows_of(t0 + i)
                        for k in range(KD):
                            dst = p[:, k * 512 + i * TT:k * 512 + i * TT + r]
                            src = xn[0:r, t0 + i, k * 128:(k + 1) * 128]
                            if kind == "xn_t":
                                ins = pe.transpose(dst, src, ident[0:r, 0:r])
                            else:
                                ins = pe.matmul(dst, src, tri[0:r, 0:r], start=True, stop=True)
                elif kind == "z":
                    c0, c1 = group_cols(n)
                    drained(pe, "zx_t", n)
                    for k in range(KD):
                        ins = pe.matmul(p[:, 0:c1 - c0], xt_pad[:, k, :], zx_t[:, k, c0:c1], start=k == 0, stop=k == KD - 1)
                elif kind == "ac":
                    c0, c1 = group_cols(n)
                    drained(pe, "xn_t", n)
                    for m, (w, src) in enumerate(((m_a, xn_t), (m_c, zx_t))):
                        for k in range(KD):
                            ins = pe.matmul(p[:, m * 512:m * 512 + c1 - c0], w[:, k, :], src[:, k, c0:c1],
                                            start=k == 0, stop=k == KD - 1)
                elif kind == "y":
                    c0, c1 = group_cols(n)
                    drained(pe, "ac", n)
                    for k in range(KD):
                        ins = pe.matmul(p[:, k * 512:k * 512 + c1 - c0], uw[:, k * 128:(k + 1) * 128], prod[:, c0:c1],
                                        start=True, stop=True)
                elif kind == "prefix":
                    pe.wait_ge(chosen_ready, 1)
                    out_p = p[0:TT, 0:NE * NT]
                    pe.matmul(out_p, neg_prefix, route[7][:, :, :].rearrange("p e t -> p (e t)"), start=True, stop=False)
                    ins = pe.matmul(out_p, ones[:, :], so_far[:, :, :].rearrange("p e t -> p (e t)"), start=False, stop=True)
                ins.then_inc(psum_filled, 1)

            def look_up(e, q):
                pe.wait_ge(onehot_ready, e + 1)
                for s in range(SLOT_TILES):
                    for t in range(NT):
                        ins = pe.matmul(bank(5)[0:ST, 400 + 3 * s:403 + 3 * s], onehot[q][:, t, s * ST:(s + 1) * ST],
                                        ids[:, t, :], start=t == 0, stop=t == NT - 1)
                ins.then_inc(info_ready, 1)

            def turn_in(e, q):
                pe.wait_ge(gathered[q], 16 * (e - q) + 32)
                for k in range(KD):
                    for s in range(SLOT_TILES):
                        ins = pe.transpose(bank(5)[:, k * SL + s * ST:k * SL + (s + 1) * ST],
                                           rows_in[q][:, s, k * 128:(k + 1) * 128], ident[0:ST, 0:ST])
                ins.then_inc(in_turned, 1)

            def up(e, q, pair, reused):
                if pair == 0:
                    pe.wait_ge(w1_in[q], 8 * (e - q) + 16)
                    pe.wait_ge(buf_ready, e + 1)
                if reused:
                    pe.wait_ge(hid_ready, (e - 1) * PAIRS + pair + 1)
                for f in (2 * pair, 2 * pair + 1):
                    for k in range(KD):
                        ins = pe.matmul(bank(pair)[:, (f % 2) * SL:(f % 2 + 1) * SL], w1_s[q][:, k, f * 128:(f + 1) * 128],
                                        buf_t[q][:, k, :], start=k == 0, stop=k == KD - 1)
                ins.then_inc(up_done, 1)

            def down(e, q, d, blocks):
                for f in blocks:
                    if d == 0 and f % 2 == 0:
                        pe.wait_ge(hid_ready, e * PAIRS + f // 2 + 1)
                    ins = pe.matmul(bank(4)[:, d * SL:(d + 1) * SL], w2_s[q][:, f, d * 128:(d + 1) * 128], hid[:, f, :],
                                    start=f == 0, stop=f == KF - 1)
                if d == KD - 1 and KF - 1 in blocks:
                    ins.then_inc(down_done, 1)

            def turn_out(e):
                pe.wait_ge(out_t_ready, e + 1)
                for s in range(SLOT_TILES):
                    for k in range(KD):
                        ins = pe.transpose(bank(6)[0:ST, s * D + k * 128:s * D + (k + 1) * 128],
                                           out_t[:, k, s * ST:(s + 1) * ST], ident)
                ins.then_inc(out_turned, 1)

            def expert(e, q, first=False, last=False):
                up(e, q, 0, not first)
                if not first:
                    turn_out(e - 1)
                for pair in range(1, PAIRS - 1):
                    up(e, q, pair, not first)
                if not last:
                    look_up(e + 1, 1 - q)
                up(e, q, PAIRS - 1, not first)
                pe.wait_ge(w2_in[q], 8 * (e - q) + 16)
                down(e, q, 0, range(KF))
                down(e, q, 1, range(KF // 2))
                if not last:
                    turn_in(e + 1, 1 - q)
                down(e, q, 1, range(KF // 2, KF))

            drained(pe, "norm2", len(GROUPS) - 1)
            look_up(0, 0)
            turn_in(0, 0)
            expert(0, 0, first=True)
            with pe.Fori(0, NE // 2 - 1) as i:
                for j in range(2):
                    expert(2 * i + 1 + j, 1 - j)
            expert(NE - 1, 1, last=True)
            turn_out(NE - 1)


_INS = ["x", "L0_tok_W", "L0_tok_b", "L0_tok_cls_token", "L0_tok_pos_enc", "L0_attn_Wq", "L0_attn_Wk", "L0_attn_Wo",
        "L0_attn_U_b", "L0_attn_V_b", "L0_attn_W_b", "L0_attn_bias_b", "L0_attn_U_t", "L0_attn_V_t", "L0_attn_W_t",
        "L0_attn_X_t", "L0_attn_bias_t", "L0_attn_alpha", "L0_ffn_w_router", "L0_ffn_b_router", "L0_ffn_w1",
        "L0_ffn_b1", "L0_ffn_w2", "L0_ffn_b2"]


def kernel(**inputs):
    import concourse.bacc as bacc
    from concourse.bass_utils import run_bass_kernel_spmd

    nc = bacc.Bacc("TRN2", target_bir_lowering=False, num_devices=1)
    arrays, args = {}, []
    for name in _INS:
        a = np.ascontiguousarray(inputs[name])
        a = a.reshape(a.shape or (1,))
        arrays[f"in_{name}"] = a
        args.append(nc.dram_tensor(f"in_{name}", a.shape, mybir.dt.from_np(a.dtype), kind="ExternalInput").ap())
    arrays["in_const"] = constants()
    args.append(nc.dram_tensor("in_const", (128, C_END), mybir.dt.float32, kind="ExternalInput").ap())
    args.append(nc.dram_tensor("xrows", (N, ROW), mybir.dt.float32).ap())
    args.append(nc.dram_tensor("out_rows", (N + SL, D), mybir.dt.float32, kind="ExternalOutput").ap())
    vit_block(nc, *args)
    got = run_bass_kernel_spmd(nc, [arrays], core_ids=[0]).results[0]["out_rows"]
    return got[:N].reshape(B, T, D)
```

```python
import concourse.bass as bass
from concourse import mybir
from contextlib import ExitStack
import numpy as np

B, CH, IMG, PATCH = 32, 3, 96, 16
NP_ = IMG // PATCH
T = NP_ * NP_ + 1
N = B * T
D = 256
KD = D // 128
R = 64
NE, F = 8, 1024
KF = F // 128
CAP = max(1, int(1.25 * N / NE))
SLOT_TILES = 2
ST = -(-CAP // SLOT_TILES)
PAIRS = KF // 2
SL = ST * SLOT_TILES
TB = 3
TT = TB * T
NT = -(-N // TT)
LAST = N - (NT - 1) * TT
KP = CH * PATCH * PATCH // 128
GROUPS = [(0, 3), (3, 3), (6, 3), (9, 2)]
PATCHES = [(t0 * TB, min(B, (t0 + n) * TB)) for t0, n in GROUPS]
EPS = 1e-5
NP2 = T - 1
VECS = T + 4
FLOOR = -87.5
INFO = 6

def layout(*widths):
    ends = np.cumsum(widths)
    return [slice(int(e - w), int(e)) for w, e in zip(widths, ends)]


C_ID, C_TRI, C_NEG, C_IOTA, C_IOTA8, C_IDS, C_OUTSIDE, C_TRASH, C_LOW, C_EPS = layout(
    128, TT, TT, SL, NE, 3 * NT, NT, SLOT_TILES, 1, 1)
A_WQ, A_WK, A_WO, A_V, A_W, A_U, A_X = layout(KD * D, KD * D, KD * D, *(4 * [KD * 2 * R]))
V_VEC, V_B1, V_B2, V_WR, V_ALPHA, V_BR = layout(KD * VECS, NE * KF, NE * KD, KD * NE, 1, NE)


def constants():
    c = np.zeros((128, C_EPS.stop), np.float32)
    c[:, C_ID] = np.eye(128)
    m, n = np.arange(TT)[:, None], np.arange(TT)[None, :]
    c[:TT, C_TRI] = np.where((m // T == n // T) & (m <= n), 1.0 / (n % T + 1), 0.0)
    c[:TT, C_NEG] = np.where(m >= n, -1.0, 0.0)
    c[:, C_IOTA] = np.where(np.arange(SL) < CAP, np.arange(SL) + 1, -5)
    c[:, C_IOTA8] = np.arange(NE)
    p, t = np.arange(128)[:, None], np.arange(NT)[None, :]
    c[:, C_IDS] = np.stack([p + 0 * t, 0 * p + t, 0 * p + 0 * t + 1], -1).reshape(128, -1)
    c[:, C_OUTSIDE] = np.where((p < TT) & (t * TT + p < N), 0, 100)
    c[:, C_TRASH] = N + p + ST * np.arange(SLOT_TILES)[None, :]
    c[:, C_LOW] = np.arange(128)[:, None] < R
    c[:, C_EPS] = EPS
    return c


def blocks(a):
    return a.reshape(-1, 128, a.shape[-1]).transpose(1, 0, 2).reshape(128, -1)


def vit_block(nc, patches, tok_w, const, vectors, attn, w1, w2, xrows, out):
    f32, bf16, i32, u32 = mybir.dt.float32, mybir.dt.bfloat16, mybir.dt.int32, mybir.dt.uint32
    ALU, ACT, AX = mybir.AluOpType, mybir.ActivationFunctionType, mybir.AxisListType

    with ExitStack() as ctx:
        def sb(name, shape, dt=f32):
            return ctx.enter_context(nc.sbuf_tensor(name, shape, dt))

        def sem(name):
            return ctx.enter_context(nc.semaphore(name))

        cst = sb("cst", [128, C_EPS.stop])
        ident = cst[:, C_ID]
        tri = cst[0:TT, C_TRI]
        iota_slot = cst[0:TT, C_IOTA]
        iota_e = cst[0:TT, C_IOTA8]
        ids = cst[0:TT, C_IDS]
        outside = cst[0:TT, C_OUTSIDE]
        trash = cst[0:ST, C_TRASH]
        eps_col = cst[:, C_EPS]
        low_rows = cst[:, C_LOW]

        def wide(ap, k=KD):
            return ap.rearrange("p (k n) -> p k n", k=k)

        vecs = sb("vecs", [128, V_BR.stop])
        vec_t = wide(vecs[:, V_VEC])
        b1_t, b2_t = vecs[:, V_B1], vecs[:, V_B2]
        wr_s = wide(vecs[:, V_WR])
        alpha_s = vecs[:, V_ALPHA]
        b_router_s = vecs[0:TT, V_BR]
        att = sb("att", [128, A_X.stop])
        wq_s, wk_s, wo_t, v_cat, w_cat, u_cat, xt_pad = (
            wide(att[:, c]) for c in (A_WQ, A_WK, A_WO, A_V, A_W, A_U, A_X))

        patch_t = sb("patch_t", [128, KP * B * NP2])
        tok_wt = sb("tok_wt", [128, KP, D])
        h_t = sb("h_t", [128, KD, N])
        h2_t = sb("h2_t", [128, KD, N])
        xn_t = sb("xn_t", [128, KD, N])
        zx_t = sb("zx_t", [128, KD, N])
        z_s = sb("z_s", [128, N])
        prod = sb("prod", [128, N])
        xn = sb("xn", [TT, NT, D])
        h2 = sb("h2", [TT, NT, D])
        onehot = [sb(f"onehot{q}", [TT, NT, SL], bf16) for q in range(2)]
        rows_in = [sb(f"rows_in{q}", [ST, SLOT_TILES, D]) for q in range(2)]
        buf_t = [sb(f"buf_t{q}", [128, KD, SL]) for q in range(2)]
        hid = sb("hid", [128, KF, SL])
        out_t = sb("out_t", [128, KD, SL])
        out_s = [sb(f"out_s{q}", [ST, SLOT_TILES, D]) for q in range(2)]
        w1_s = [sb(f"w1_s{q}", [128, KD, F]) for q in range(2)]
        w2_s = [sb(f"w2_s{q}", [128, KF, D]) for q in range(2)]
        m_a = sb("m_a", [128, KD, 2 * R])
        m_c = sb("m_c", [128, KD, 2 * R])
        uw = sb("uw", [128, D])
        u_scale = sb("u_scale", [128, 1])
        bias_s = sb("bias_s", [128, KD])
        bias_o = sb("bias_o", [128, KD])
        table = sb("table", [128, KD, T])
        wr_c = sb("wr_c", [128, KD, NE])
        mean_mat = sb("mean_mat", [128, 128])
        ones = sb("ones", [TT, TT], bf16)
        neg_prefix = sb("neg_prefix", [TT, TT], bf16)
        zeros = sb("zeros", [ST, SLOT_TILES * D])
        bn = sb("bn", [TT, 3, 6])
        mv = sb("mv", [TT, 2 * NT, 2])
        rstd = sb("rstd", [TT, 2 * NT])
        std = sb("std", [TT, 2 * NT])
        nmr = sb("nmr", [TT, 2 * NT])
        logit = sb("logit", [TT, NT, NE])
        below = sb("below", [TT, NT, NE])
        floored = sb("floored", [TT, NT, NE])
        top = sb("top", [TT, NT, 8])
        top2 = sb("top2", [TT, NT, 8])
        which = sb("which", [TT, NT, 8], u32)
        which_f = sb("which_f", [TT, NT, 2])
        is_one = sb("is_one", [TT, NT, 2, NE])
        chosen = sb("chosen", [TT, NT, NE], bf16)
        before = sb("before", [TT, len(GROUPS) + 1, NE], bf16)
        group_sum = sb("group_sum", [TT, NE])
        kept = sb("kept", [TT, NT, NE])
        dest = sb("dest", [TT, NT, NE])
        expd = sb("expd", [TT, NT, NE])
        weight = sb("weight", [TT, NT, NE])
        part = sb("part", [TT, NT, NE], bf16)
        col = [sb(f"col{n}", [TT, NT]) for n in range(6)]
        marks = sb("marks", [TT, NT, NE, INFO], bf16)
        info = [sb(f"info{q}", [ST, SLOT_TILES, INFO]) for q in range(2)]
        slot_c = sb("slot_c", [ST, SLOT_TILES])
        slot_a = sb("slot_a", [ST, SLOT_TILES])
        slot_b = sb("slot_b", [ST, SLOT_TILES])
        src_row = [sb(f"src_row{q}", [ST, SLOT_TILES], i32) for q in range(2)]
        b1_cur = [sb(f"b1_cur{q}", [128, KF]) for q in range(2)]
        b2_cur = [sb(f"b2_cur{q}", [128, KD]) for q in range(2)]
        coef_cur = [sb(f"coef_cur{q}", [ST, SLOT_TILES]) for q in range(2)]
        dst_row = [sb(f"dst_row{q}", [ST, SLOT_TILES], i32) for q in range(2)]

        ps = ctx.enter_context(nc.psum_tensor("ps", [128, 8 * 512], f32))

        def slot(u):
            return ps[:, (u % 4) * 1024:(u % 4 + 1) * 1024]

        def bank(b):
            return ps[:, b * 512:(b + 1) * 512]

        const_in, attn_in, vec_in = sem("const_in"), sem("attn_in"), sem("vec_in")
        tok_w_in = [sem(f"tok_w_in{h}") for h in range(2)]
        patch_in = [sem(f"patch_in{g}") for g in range(len(GROUPS) + 1)]
        pool_set = sem("pool_set")
        psum_filled = sem("psum_filled")
        dve_drained = sem("dve_drained")
        act_drained = sem("act_drained")
        dve_step = sem("dve_step")
        var_ready, std_ready = sem("var_ready"), sem("std_ready")
        stats1_ready, stats2_ready = sem("stats1_ready"), sem("stats2_ready")
        rows_stored = [sem(f"rows_stored{g}") for g in range(len(GROUPS))]
        out_stored = sem("out_stored")
        added = sem("added")
        out_free = sem("out_free")
        below_ready, exp_ready = sem("below_ready"), sem("exp_ready")
        chosen_ready, weights_ready, weights_looked = sem("chosen_ready"), sem("weights_ready"), sem("weights_looked")
        w1_in = [sem(f"w1_in{q}") for q in range(2)]
        w2_in = [sem(f"w2_in{q}") for q in range(2)]
        onehot_ready, info_ready, src_ready, dst_ready = (
            sem(n) for n in ("onehot_ready", "info_ready", "src_ready", "dst_ready"))
        gathered = [sem(f"gathered{q}") for q in range(2)]
        in_turned, buf_ready = sem("in_turned"), sem("buf_ready")
        up_done, hid_ready, down_done, out_t_ready = (
            sem(n) for n in ("up_done", "hid_ready", "down_done", "out_t_ready"))
        out_turned, out_s_ready = sem("out_turned"), sem("out_s_ready")
        logits_read, biases_ready, weights_kept = sem("logits_read"), sem("biases_ready"), sem("weights_kept")
        before_ready = sem("before_ready")
        prepared = sem("prepared")
        find_step = sem("find_step")

        A, B_, C, E = range(len(GROUPS))
        UNITS = [("proj", A, "dve"), ("mac", 0, "act"), ("uw", 0, "dve"), ("proj", B_, "dve"), ("norm1", A, "act"),
                 ("proj", C, "dve"), ("xn_t", A, "dve"), ("zx_t", A, "act"), ("norm1", B_, "act"),
                 ("proj", E, "dve"), ("z", A, "act"), ("ac", A, "dve"), ("xn_t", B_, "dve"), ("zx_t", B_, "act"),
                 ("norm1", C, "act"), ("y", A, "dve"), ("z", B_, "act"), ("ac", B_, "dve"),
                 ("xn_t", C, "dve"), ("zx_t", C, "act"), ("norm1", E, "act"), ("norm2", A, "act"),
                 ("y", B_, "dve"), ("z", C, "act"), ("ac", C, "dve"), ("xn_t", E, "dve"), ("zx_t", E, "act"),
                 ("norm2", B_, "act"), ("y", C, "dve"), ("z", E, "act"), ("ac", E, "dve"), ("slots", A, "dve"),
                 ("norm2", C, "act"), ("y", E, "dve"), ("slots", B_, "dve"), ("norm2", E, "act"),
                 ("slots", C, "dve"), ("slots", E, "dve")]
        PLACE = {(kind, n): u for u, (kind, n, _) in enumerate(UNITS)}

        def drained(eng, kind, n):
            u = PLACE[kind, n]
            reader = UNITS[u][2]
            eng.wait_ge(act_drained if reader == "act" else dve_drained,
                        sum(1 for v in UNITS[:u + 1] if v[2] == reader))

        def filled(eng, kind, n):
            eng.wait_ge(psum_filled, PLACE[kind, n] + 1)
            return slot(PLACE[kind, n])

        def rows_of(t):
            return TT if t < NT - 1 else LAST

        def patch_cols(g):
            a, b = PATCHES[g]
            return KP * a * NP2, KP * b * NP2

        def group_parts(g):
            t0, n = GROUPS[g]
            return [(TT, t0, t0 + n)] if t0 + n < NT else [(TT, t0, NT - 1), (LAST, NT - 1, NT)]

        def group_cols(g):
            t0, n = GROUPS[g]
            return t0 * TT, min(N, (t0 + n) * TT)

        block = ctx.enter_context(nc.Block())

        @block.sync
        def _(sp):
            hw = KP // 2 * D
            for h in range(2):
                sp.dma_start(tok_wt[:, h * KP // 2:(h + 1) * KP // 2].rearrange("p k d -> p (k d)"),
                             tok_w[:, h * hw:(h + 1) * hw]).then_inc(tok_w_in[h], 16)
                c0, c1 = patch_cols(0)
                mid = c0 + (c1 - c0) // 2
                a, b = (c0, mid) if h == 0 else (mid, c1)
                sp.dma_start(patch_t[:, a:b], patches[:, a:b]).then_inc(patch_in[0 if h == 0 else len(GROUPS)], 16)
            sp.dma_start(vecs[:, :], vectors).then_inc(vec_in, 16)
            sp.dma_start(att[:, :], attn).then_inc(attn_in, 16)
            for g in range(1, len(GROUPS)):
                c0, c1 = patch_cols(g)
                sp.dma_start(patch_t[:, c0:c1], patches[:, c0:c1]).then_inc(patch_in[g], 16)
                if g == 1:
                    sp.dma_start(cst[:, :], const).then_inc(const_in, 16)

            def load_w1(e, q):
                sp.dma_start(w1_s[q][:, :, :], w1[e].rearrange("(k p) f -> p k f", p=128)).then_inc(w1_in[q], 16)

            def load_w2(e, q):
                sp.dma_start(w2_s[q][:, :, :], w2[e].rearrange("(k p) d -> p k d", p=128)).then_inc(w2_in[q], 16)

            for e in range(2):
                load_w1(e, e)
                load_w2(e, e)
            sp.wait_ge(pool_set, 1)
            sp.dma_start(out[N:N + SL].rearrange("(p s) d -> p (s d)", p=ST), zeros[:, :]).then_inc(out_stored, 16)

            def tile_rows(dram, t0, n):
                return dram[t0 * TT:(t0 + n) * TT].rearrange("(t p) d -> p t d", p=TT)

            for g, (t0, n) in enumerate(GROUPS):
                whole = n - (t0 + n == NT)
                drained(sp, "norm2", g)
                sp.dma_start(tile_rows(xrows, t0, whole), xn[:, t0:t0 + whole]).then_inc(rows_stored[g], 16)
                sp.dma_start(tile_rows(out, t0, whole), h2[:, t0:t0 + whole]).then_inc(out_stored, 16)
                if whole < n:
                    sp.dma_start(xrows[N - LAST:N], xn[0:LAST, NT - 1]).then_inc(rows_stored[g], 16)
                    sp.dma_start(out[N - LAST:N], h2[0:LAST, NT - 1]).then_inc(out_stored, 16)
            with sp.Fori(0, NE // 2 - 1) as i:
                for q in range(2):
                    e = 2 * i + q + 2
                    sp.wait_ge(up_done, (e - 1) * PAIRS)
                    load_w1(e, q)
                    sp.wait_ge(down_done, e - 1)
                    load_w2(e, q)

        @block.gpsimd
        def _(pool):
            pool.memset(zeros[:, :], 0.0).then_inc(pool_set, 1)
            pool.memset(mean_mat[:, :], 1.0 / D).then_inc(pool_set, 1)
            pool.memset(u_scale[:, :], 1.0).then_inc(pool_set, 1)
            pool.memset(ones[:, :], 1.0).then_inc(pool_set, 1)
            pool.memset(before[:, 0], 0.0).then_inc(pool_set, 1)
            pool.memset(logit[:, NT - 1:NT], 0.0).then_inc(pool_set, 1)

            def gather(e, q):
                pool.wait_ge(src_ready, e + 1)
                for s in range(SLOT_TILES):
                    pool.indirect_dma_start(
                        out=rows_in[q][:, s, :], out_offset=None, in_=xrows[:, :],
                        in_offset=bass.IndirectOffsetOnAxis(ap=src_row[q][:, s:s + 1], axis=0),
                    ).then_inc(gathered[q], 16)

            def add_out(e, q):
                if e == 0:
                    pool.wait_ge(out_stored, 16 * (len(GROUPS) + 2))
                else:
                    pool.wait_ge(added, e * 16 * SLOT_TILES)
                pool.sem_inc(out_free, 1)
                pool.wait_ge(dst_ready, e + 1)
                pool.wait_ge(out_s_ready, e + 1)
                for s in range(SLOT_TILES):
                    pool.indirect_dma_start(
                        out=out[:, :], out_offset=bass.IndirectOffsetOnAxis(ap=dst_row[q][:, s:s + 1], axis=0),
                        in_=out_s[q][:, s, :], in_offset=None, compute_op=ALU.add,
                    ).then_inc(added, 16)

            for g, (t0, n) in enumerate(GROUPS):
                pool.wait_ge(rows_stored[g], 16 * (1 + (t0 + n == NT)))
            gather(0, 0)
            for e in range(NE):
                if e > 0:
                    add_out(e - 1, (e - 1) % 2)
                if e < NE - 1:
                    gather(e + 1, (e + 1) % 2)
            add_out(NE - 1, (NE - 1) % 2)
            pool.wait_ge(added, NE * 16 * SLOT_TILES)

        @block.scalar
        def _(act):
            def copy(dst, src):
                return act.activation(dst, src, ACT.Copy)

            stds = [0]

            def take_roots(g, base):
                stds[0] += 1
                act.wait_ge(var_ready, stds[0])
                for r, a, b in group_parts(g):
                    ins = act.activation(std[0:r, base + a:base + b], mv[0:r, base + a:base + b, 1], ACT.Sqrt,
                                         bias=eps_col[0:r])
                ins.then_inc(std_ready, 1)

            def norm1(g):
                take_roots(g, 0)
                act.wait_ge(stats1_ready, g + 1)
                p = slot(PLACE["norm1", g])
                t0, n = GROUPS[g]
                for i in range(n):
                    t = t0 + i
                    r = rows_of(t)
                    ins = act.activation(xn[0:r, t], p[0:r, i * D:(i + 1) * D], ACT.Identity,
                                         bias=nmr[0:r, t:t + 1], scale=rstd[0:r, t:t + 1])
                ins.then_inc(act_drained, 1)

            def norm2(g):
                take_roots(g, NT)
                act.wait_ge(stats2_ready, g + 1)
                drained(act, "xn_t", g)
                p = slot(PLACE["norm2", g])
                t0, n = GROUPS[g]
                for i in range(n):
                    t = t0 + i
                    r = rows_of(t)
                    act.activation(xn[0:r, t], p[0:r, i * D:(i + 1) * D], ACT.Identity,
                                   bias=nmr[0:r, NT + t:NT + t + 1], scale=rstd[0:r, NT + t:NT + t + 1])
                whole = n - (t0 + n == NT)
                ins = copy(h2[:, t0:t0 + whole], p[0:TT, 0:whole * D].rearrange("p (t d) -> p t d", t=whole))
                if whole < n:
                    ins = copy(h2[0:LAST, NT - 1], p[0:LAST, whole * D:n * D])
                ins.then_inc(act_drained, 1)

            for kind, n, reader in UNITS:
                if reader != "act":
                    continue
                if kind == "mac":
                    p = filled(act, kind, n)
                    act.wait_ge(const_in, 16)
                    copy(m_a[:, :, :], p[:, 0:256].rearrange("p (k r) -> p k r", k=KD))
                    copy(m_c[:, :, :], p[:, 256:512].rearrange("p (k r) -> p k r", k=KD)).then_inc(act_drained, 1)
                elif kind == "norm1":
                    norm1(n)
                elif kind == "zx_t":
                    c0, c1 = group_cols(n)
                    p = filled(act, kind, n).rearrange("p (k s) -> p k s", k=KD)
                    copy(zx_t[:, :, c0:c1], p[:, :, 0:c1 - c0]).then_inc(act_drained, 1)
                elif kind == "z":
                    c0, c1 = group_cols(n)
                    p = filled(act, kind, n)
                    act.activation(z_s[:, c0:c1], p[:, 0:c1 - c0], ACT.Identity, bias=low_rows).then_inc(act_drained, 1)
                elif kind == "norm2":
                    norm2(n)
            act.wait_ge(below_ready, len(GROUPS))
            act.activation(expd[:, :, :], below[:, :, :], ACT.Exp).then_inc(exp_ready, 1)

            def hidden(e, q, pair):
                if pair == 0:
                    act.wait_ge(biases_ready, e + 1)
                act.wait_ge(up_done, e * PAIRS + pair + 1)
                for f in (2 * pair, 2 * pair + 1):
                    ins = act.activation(hid[:, f, :], bank(pair)[:, (f % 2) * SL:(f % 2 + 1) * SL], ACT.Gelu,
                                         bias=b1_cur[q][:, f:f + 1])
                ins.then_inc(hid_ready, 1)

            def weigh(e, q):
                act.wait_ge(out_turned, e + 1)
                act.wait_ge(dst_ready, e + 1)
                act.wait_ge(out_free, e + 1)
                for s in range(SLOT_TILES):
                    ins = act.activation(out_s[q][:, s, :], bank(6)[0:ST, s * D:(s + 1) * D], ACT.Copy,
                                         scale=coef_cur[q][:, s:s + 1])
                ins.then_inc(out_s_ready, 1)

            for pair in range(PAIRS):
                hidden(0, 0, pair)
            with act.Fori(0, NE // 2 - 1) as i:
                for j in range(2):
                    e = 2 * i + 1 + j
                    hidden(e, 1 - j, 0)
                    weigh(e - 1, j)
                    for pair in range(1, PAIRS):
                        hidden(e, 1 - j, pair)
            hidden(NE - 1, 1, 0)
            weigh(NE - 2, 0)
            for pair in range(1, PAIRS):
                hidden(NE - 1, 1, pair)
            weigh(NE - 1, 1)

        @block.vector
        def _(dve):
            steps, stds = [0], [0]

            def step(ins):
                steps[0] += 1
                ins.then_inc(dve_step, 1)
                dve.wait_ge(dve_step, steps[0])

            def read_logits(p, g):
                t0, c = GROUPS[g]
                for i in range(c):
                    t, r = t0 + i, rows_of(t0 + i)
                    ins = dve.scalar_tensor_tensor(logit[0:r, t], p[0:r, 3 * D + i * NE:3 * D + (i + 1) * NE],
                                                   rstd[0:r, NT + t:NT + t + 1], b_router_s[0:r], ALU.mult, ALU.add)
                ins.then_inc(logits_read, 1)

            def stats(p, g, base, ready, read_rest=None):
                t0, n = GROUPS[g]
                for i in range(n):
                    r = rows_of(t0 + i)
                    ins = dve.bn_stats(bn[0:r, i], p[0:r, i * D:(i + 1) * D])
                step(ins)
                for i in range(n):
                    r = rows_of(t0 + i)
                    ins = dve.bn_aggr(mv[0:r, base + t0 + i], bn[0:r, i])
                ins.then_inc(var_ready, 1)
                stds[0] += 1
                parts = group_parts(g)
                dve.wait_ge(std_ready, stds[0])
                for r, a, b in parts:
                    ins = dve.reciprocal(rstd[0:r, base + a:base + b], std[0:r, base + a:base + b])
                step(ins)
                if read_rest is not None:
                    read_rest(p, g)
                for r, a, b in parts:
                    ins = dve.scalar_tensor_tensor(nmr[0:r, base + a:base + b], mv[0:r, base + a:base + b, 0], -1.0,
                                                   rstd[0:r, base + a:base + b], ALU.mult, ALU.mult)
                ins.then_inc(ready, 1)

            dve.wait_ge(vec_in, 16)
            dve.wait_ge(pool_set, 6)
            step(dve.scalar_tensor_tensor(bias_s[:, :], vec_t[:, :, T + 3], alpha_s, vec_t[:, :, T + 2],
                                          ALU.mult, ALU.add))
            for k in range(KD):
                dve.tensor_scalar(table[:, k, 1:T], vec_t[:, k, 1:T], vec_t[:, k, T + 1:T + 2], None, ALU.add)
            dve.tensor_tensor(table[:, :, 0:1], vec_t[:, :, 0:1], vec_t[:, :, T:T + 1], ALU.add)
            step(dve.tensor_copy(u_scale[R:, :], alpha_s[R:, :]))
            step(dve.tensor_copy(h_t[:, :, :].rearrange("p k (b t) -> p k b t", t=T)[:, :, :, 0],
                                 table[:, :, 0:1].broadcast_to((128, KD, B))))
            dve.wait_ge(const_in, 16)
            dve.tensor_copy(neg_prefix[:, :], cst[0:TT, C_NEG])
            for t in range(NT):
                ins = dve.tensor_copy(marks[:, t, :, 0:3], ids[:, 3 * t:3 * t + 3].rearrange(
                    "p (a c) -> p a c", a=1).broadcast_to((TT, NE, 3)))
            ins.then_inc(prepared, 1)

            def choose(g):
                t0, n = GROUPS[g]
                tiles = range(t0, t0 + n)
                ts = slice(t0, t0 + n)
                for t in tiles:
                    ins = dve.max(top[:, t], logit[:, t])
                step(ins)
                for t in tiles:
                    ins = dve.tensor_scalar(floored[:, t], logit[:, t], top[:, t, 0:1], FLOOR, ALU.subtract, ALU.max)
                step(ins)
                for t in tiles:
                    ins = dve.max(top2[:, t], floored[:, t])
                step(ins)
                for t in tiles:
                    ins = dve.max_index(which[:, t], top2[:, t], floored[:, t])
                step(ins)
                step(dve.tensor_tensor(which_f[:, ts], which[:, ts, 0:2],
                                       outside[:, ts].rearrange("p (t a) -> p t a", a=1).broadcast_to((TT, n, 2)), ALU.add))
                step(dve.tensor_tensor(is_one[:, ts],
                                       iota_e.rearrange("p (a b e) -> p a b e", a=1, b=1).broadcast_to((TT, n, 2, NE)),
                                       which_f[:, ts].rearrange("p t (k a) -> p t k a", a=1).broadcast_to((TT, n, 2, NE)),
                                       ALU.is_equal))
                dve.tensor_tensor(chosen[:, ts], is_one[:, ts, 0], is_one[:, ts, 1], ALU.add).then_inc(chosen_ready, 1)
                dve.tensor_tensor(below[:, ts], logit[:, ts], top[:, ts, 0:1].broadcast_to((TT, n, NE)),
                                  ALU.subtract).then_inc(below_ready, 1)
                dve.wait_ge(chosen_ready, g + 1)
                step(dve.tensor_reduce(group_sum[:, :], chosen[:, ts].rearrange("p t e -> p e t"), AX.X, ALU.add))
                dve.tensor_tensor(before[:, g + 1], before[:, g], group_sum[:, :], ALU.add).then_inc(before_ready, 1)
                dve.wait_ge(before_ready, g + 1)

            def find_part(g):
                t0, n = GROUPS[g]
                return dve.tensor_tensor(onehot[0][:, t0:t0 + n],
                                         iota_slot.rearrange("p (a s) -> p a s", a=1).broadcast_to((TT, n, SL)),
                                         dest[:, t0:t0 + n, 0:1].broadcast_to((TT, n, SL)), ALU.is_equal)

            for kind, n, reader in UNITS:
                if kind == "norm1":
                    stats(filled(dve, kind, n), n, 0, stats1_ready)
                    continue
                if kind == "norm2":
                    p = filled(dve, kind, n)
                    stats(p, n, NT, stats2_ready, read_logits)
                    dve.wait_ge(logits_read, n + 1)
                    choose(n)
                    continue
                if reader != "dve":
                    continue
                if kind == "mac":
                    pass
                elif kind == "uw":
                    p = filled(dve, kind, n)
                    dve.tensor_scalar(uw[:, :], p[:, 0:D], u_scale[:, 0:1], None, ALU.mult)
                    for k in range(KD):
                        dve.tensor_tensor(wr_c[:, k], wr_s[:, k], p[:, 264:264 + NE], ALU.subtract)
                    dve.tensor_copy(bias_o[:, :], p[:, 256:256 + KD]).then_inc(dve_drained, 1)
                elif kind == "proj":
                    p = filled(dve, kind, n)
                    b0, b1_ = PATCHES[n]
                    nb = b1_ - b0
                    for k in range(KD):
                        dst = h_t[:, k, b0 * T:b1_ * T].rearrange("p (b t) -> p b t", t=T)[:, :, 1:T]
                        src = p[:, k * 512:k * 512 + nb * NP2].rearrange("p (b t) -> p b t", t=NP2)
                        ins = dve.tensor_tensor(dst, src, table[:, k:k + 1, 1:T].broadcast_to((128, nb, NP2)), ALU.add)
                    ins.then_inc(dve_drained, 1)
                elif kind == "xn_t":
                    c0, c1 = group_cols(n)
                    p = filled(dve, kind, n).rearrange("p (k s) -> p k s", k=KD)
                    dve.tensor_copy(xn_t[:, :, c0:c1], p[:, :, 0:c1 - c0]).then_inc(dve_drained, 1)
                elif kind == "ac":
                    c0, c1 = group_cols(n)
                    p = filled(dve, kind, n)
                    drained(dve, "z", n)
                    step(dve.tensor_tensor(z_s[:, c0:c1], p[:, 512:512 + c1 - c0], z_s[:, c0:c1], ALU.mult))
                    dve.tensor_tensor(prod[:, c0:c1], p[:, 0:c1 - c0], z_s[:, c0:c1], ALU.mult).then_inc(dve_drained, 1)
                elif kind == "y":
                    c0, c1 = group_cols(n)
                    p = filled(dve, kind, n)
                    for k in range(KD):
                        ins = dve.scalar_tensor_tensor(h2_t[:, k, c0:c1], p[:, k * 512:k * 512 + c1 - c0], bias_o[:, k:k + 1],
                                                       h_t[:, k, c0:c1], ALU.add, ALU.add)
                    ins.then_inc(dve_drained, 1)
                elif kind == "slots":
                    t0, c = GROUPS[n]
                    ts = slice(t0, t0 + c)
                    p = filled(dve, kind, n)[0:TT, 0:c * NE].rearrange("p (t e) -> p t e", e=NE)
                    step(dve.scalar_tensor_tensor(dest[:, ts], p, 1.0, chosen[:, ts], ALU.add, ALU.mult))
                    if n == len(GROUPS) - 1:
                        find_part(n).then_inc(onehot_ready, 1)
                    else:
                        find_part(n)
                    dve.scalar_tensor_tensor(kept[:, ts], p, float(CAP), chosen[:, ts], ALU.is_lt, ALU.mult
                                             ).then_inc(dve_drained, 1)

            def weigh_tokens():
                every, of_all, rs, got, ws, rw = (c[:, :] for c in col)

                def per_token(c):
                    return c.rearrange("p (t a) -> p t a", a=1).broadcast_to((TT, NT, NE))

                dve.wait_ge(exp_ready, 1)
                dve.tensor_reduce(every, expd[:, :, :], AX.X, ALU.add)
                step(dve.tensor_tensor(weight[:, :, :], expd[:, :, :], kept[:, :, :], ALU.mult))
                dve.tensor_reduce(got, weight[:, :, :], AX.X, ALU.add)
                step(dve.reciprocal(rs, every))
                step(dve.tensor_tensor(ws, got, rs, ALU.mult))
                step(dve.tensor_scalar(ws, ws, 1e-6, None, ALU.max))
                step(dve.reciprocal(rw, ws))
                step(dve.tensor_tensor(rw, rw, rs, ALU.mult))
                step(dve.tensor_tensor(weight[:, :, :], weight[:, :, :], per_token(rw), ALU.mult))
                step(dve.tensor_copy(marks[:, :, :, 3], weight[:, :, :]))
                step(dve.tensor_tensor(weight[:, :, :], weight[:, :, :], marks[:, :, :, 3], ALU.subtract))
                step(dve.tensor_copy(marks[:, :, :, 4], weight[:, :, :]))
                step(dve.tensor_tensor(weight[:, :, :], weight[:, :, :], marks[:, :, :, 4], ALU.subtract))
                dve.tensor_copy(marks[:, :, :, 5], weight[:, :, :]).then_inc(weights_ready, 1)

            def find(e, q):
                dve.tensor_tensor(onehot[q][:, :, :], iota_slot.rearrange("p (a s) -> p a s", a=1).broadcast_to((TT, NT, SL)),
                                  dest[:, :, bass.ds(e, 1)].broadcast_to((TT, NT, SL)), ALU.is_equal).then_inc(onehot_ready, 1)

            def looked_up(c0, c1, b=5):
                return bank(b)[0:ST, 400:400 + INFO * SLOT_TILES].rearrange("p (s c) -> p s c", c=INFO)[:, :, c0:c1]

            def rows(e, q, c1=INFO):
                dve.wait_ge(info_ready, e + 1)
                dve.tensor_copy(info[q][:, :, 0:c1], looked_up(0, c1)).then_inc(find_step, 1)
                dve.wait_ge(find_step, 2 * e + 1)
                dve.scalar_tensor_tensor(src_row[q][:, :], info[q][:, :, 1], float(TT), info[q][:, :, 0],
                                         ALU.mult, ALU.add).then_inc(src_ready, 1)

            def settle(e, q, reused):
                dve.scalar_tensor_tensor(slot_a[:, :], info[q][:, :, 1], float(TT), info[q][:, :, 0], ALU.mult, ALU.add)
                dve.scalar_tensor_tensor(slot_b[:, :], info[q][:, :, 2], 0.0, trash, ALU.is_equal, ALU.mult)
                dve.tensor_tensor(slot_c[:, :], info[q][:, :, 3], info[q][:, :, 4], ALU.add).then_inc(find_step, 1)
                dve.wait_ge(find_step, 2 * e + 2)
                if reused:
                    dve.wait_ge(added, (e - 1) * 16 * SLOT_TILES)
                dve.tensor_tensor(coef_cur[q][:, :], slot_c[:, :], info[q][:, :, 5], ALU.add)
                dve.tensor_tensor(dst_row[q][:, :], slot_a[:, :], slot_b[:, :], ALU.add).then_inc(dst_ready, 1)

            def take_in(e, q):
                dve.wait_ge(in_turned, e + 1)
                dve.tensor_copy(buf_t[q][:, :, :], wide(bank(5)[:, 0:KD * SL])).then_inc(buf_ready, 1)
                dve.tensor_copy(b1_cur[q][:, :], b1_t[:, bass.ds(e * KF, KF)])
                dve.tensor_copy(b2_cur[q][:, :], b2_t[:, bass.ds(e * KD, KD)]).then_inc(biases_ready, 1)

            def read_out(e, q):
                dve.wait_ge(down_done, e + 1)
                for k in range(KD):
                    ins = dve.tensor_scalar(out_t[:, k, :], bank(4)[:, k * SL:(k + 1) * SL], b2_cur[q][:, k:k + 1],
                                            None, ALU.add)
                ins.then_inc(out_t_ready, 1)

            rows(0, 0, 3)
            weigh_tokens()
            take_in(0, 0)
            find(1, 1)
            dve.wait_ge(weights_looked, 1)
            dve.tensor_copy(info[0][:, :, 3:INFO], looked_up(3, INFO, 7)).then_inc(weights_kept, 1)
            dve.wait_ge(weights_kept, 1)
            settle(0, 0, False)
            rows(1, 1)
            take_in(1, 1)
            read_out(0, 0)
            settle(1, 1, False)
            with dve.Fori(0, NE // 2 - 1) as i:
                for j in range(2):
                    e = 2 * i + 1 + j
                    find(e + 1, j)
                    rows(e + 1, j)
                    take_in(e + 1, j)
                    read_out(e, 1 - j)
                    settle(e + 1, j, True)
            read_out(NE - 1, 1)

        @block.tensor
        def _(pe):
            def claim(u):
                if u >= 4:
                    drained(pe, *UNITS[u - 4][:2])

            for u, (kind, n, _reader) in enumerate(UNITS):
                claim(u)
                p = slot(u)
                if kind == "mac":
                    pe.wait_ge(attn_in, 16)
                    for m, (w, v) in enumerate(((wq_s, v_cat), (wk_s, w_cat))):
                        for d in range(KD):
                            for k in range(KD):
                                o = m * 256 + d * 128
                                ins = pe.matmul(p[:, o:o + 128], w[:, k, d * 128:(d + 1) * 128], v[:, k, :],
                                                start=k == 0, stop=k == KD - 1)
                elif kind == "uw":
                    pe.wait_ge(dve_step, 1)
                    pe.wait_ge(vec_in, 16)
                    pe.wait_ge(pool_set, 2)
                    for k in range(KD):
                        pe.matmul(p[:, 0:D], u_cat[:, k, :], wo_t[:, k, :], start=k == 0, stop=k == KD - 1)
                    for o in range(KD):
                        for k in range(KD):
                            pe.matmul(p[:, 256 + o:257 + o], wo_t[:, k, o * 128:(o + 1) * 128], bias_s[:, k:k + 1],
                                      start=k == 0, stop=k == KD - 1)
                    for k in range(KD):
                        ins = pe.matmul(p[:, 264:264 + NE], mean_mat[:, :], wr_s[:, k, :], start=k == 0, stop=k == KD - 1)
                elif kind == "proj":
                    nb = PATCHES[n][1] - PATCHES[n][0]
                    src = wide(patch_t[:, slice(*patch_cols(n))], KP)
                    for h in range(2):
                        pe.wait_ge(tok_w_in[h], 16)
                        pe.wait_ge(patch_in[n if h == 0 or n else len(GROUPS)], 16)
                        for d in range(KD):
                            for k in range(h * KP // 2, (h + 1) * KP // 2):
                                ins = pe.matmul(p[:, d * 512:d * 512 + nb * NP2], tok_wt[:, k, d * 128:(d + 1) * 128],
                                                src[:, k, :], start=k == 0, stop=k == KP - 1)
                elif kind in ("norm1", "norm2"):
                    src = h_t if kind == "norm1" else h2_t
                    if kind == "norm1":
                        pe.wait_ge(const_in, 16)
                        pe.wait_ge(dve_step, 3)
                        drained(pe, "proj", n)
                    else:
                        drained(pe, "y", n)
                    t0, c = GROUPS[n]
                    for i in range(c):
                        r = rows_of(t0 + i)
                        cols = slice((t0 + i) * TT, (t0 + i) * TT + r)
                        for k in range(KD):
                            ins = pe.transpose(p[0:r, i * D + k * 128:i * D + (k + 1) * 128], src[:, k, cols], ident)
                        if kind == "norm2":
                            drained(pe, "uw", 0)
                            for k in range(KD):
                                ins = pe.matmul(p[0:r, 3 * D + i * NE:3 * D + (i + 1) * NE], src[:, k, cols], wr_c[:, k, :],
                                                start=k == 0, stop=k == KD - 1)
                elif kind in ("xn_t", "zx_t"):
                    drained(pe, "norm1", n)
                    t0, c = GROUPS[n]
                    for i in range(c):
                        r = rows_of(t0 + i)
                        for k in range(KD):
                            dst = p[:, k * 512 + i * TT:k * 512 + i * TT + r]
                            src = xn[0:r, t0 + i, k * 128:(k + 1) * 128]
                            if kind == "xn_t":
                                ins = pe.transpose(dst, src, ident[0:r, 0:r])
                            else:
                                ins = pe.matmul(dst, src, tri[0:r, 0:r], start=True, stop=True)
                elif kind == "z":
                    c0, c1 = group_cols(n)
                    drained(pe, "zx_t", n)
                    for k in range(KD):
                        ins = pe.matmul(p[:, 0:c1 - c0], xt_pad[:, k, :], zx_t[:, k, c0:c1], start=k == 0, stop=k == KD - 1)
                elif kind == "ac":
                    c0, c1 = group_cols(n)
                    drained(pe, "xn_t", n)
                    for m, (w, src) in enumerate(((m_a, xn_t), (m_c, zx_t))):
                        for k in range(KD):
                            ins = pe.matmul(p[:, m * 512:m * 512 + c1 - c0], w[:, k, :], src[:, k, c0:c1],
                                            start=k == 0, stop=k == KD - 1)
                elif kind == "y":
                    c0, c1 = group_cols(n)
                    drained(pe, "ac", n)
                    for k in range(KD):
                        ins = pe.matmul(p[:, k * 512:k * 512 + c1 - c0], uw[:, k * 128:(k + 1) * 128], prod[:, c0:c1],
                                        start=True, stop=True)
                elif kind == "slots":
                    pe.wait_ge(chosen_ready, n + 1)
                    pe.wait_ge(prepared, 1)
                    pe.wait_ge(before_ready, n) if n else None
                    t0, c = GROUPS[n]
                    own = chosen[:, t0:t0 + c].rearrange("p t e -> p (t e)")
                    pe.matmul(p[0:TT, 0:c * NE], neg_prefix[:, :], own, start=True, stop=False)
                    for lag in range(c):
                        pe.matmul(p[0:TT, lag * NE:c * NE], ones[:, :], own[:, 0:(c - lag) * NE], start=False, stop=False)
                    ins = pe.matmul(p[0:TT, 0:c * NE], ones[:, :], before[:, n:n + 1].broadcast_to((TT, c, NE)),
                                    start=False, stop=True)
                ins.then_inc(psum_filled, 1)

            def look_up(e, q, c0=0, c1=INFO, b=5):
                pe.wait_ge(onehot_ready, e + 1)
                for s in range(SLOT_TILES):
                    for t in range(NT):
                        ins = pe.matmul(bank(b)[0:ST, 400 + INFO * s + c0:400 + INFO * s + c1],
                                        onehot[q][:, t, s * ST:(s + 1) * ST], marks[:, t, bass.ds(e, 1), c0:c1],
                                        start=t == 0, stop=t == NT - 1)
                return ins

            def turn_in(e, q):
                pe.wait_ge(gathered[q], 16 * (e - q) + 32)
                for k in range(KD):
                    for s in range(SLOT_TILES):
                        ins = pe.transpose(bank(5)[:, k * SL + s * ST:k * SL + (s + 1) * ST],
                                           rows_in[q][:, s, k * 128:(k + 1) * 128], ident[0:ST, 0:ST])
                ins.then_inc(in_turned, 1)

            def up(e, q, pair, reused):
                if pair == 0:
                    pe.wait_ge(w1_in[q], 8 * (e - q) + 16)
                    pe.wait_ge(buf_ready, e + 1)
                if reused:
                    pe.wait_ge(hid_ready, (e - 1) * PAIRS + pair + 1)
                for f in (2 * pair, 2 * pair + 1):
                    for k in range(KD):
                        ins = pe.matmul(bank(pair)[:, (f % 2) * SL:(f % 2 + 1) * SL], w1_s[q][:, k, f * 128:(f + 1) * 128],
                                        buf_t[q][:, k, :], start=k == 0, stop=k == KD - 1)
                ins.then_inc(up_done, 1)

            def down(e, q, d, blocks):
                for f in blocks:
                    if d == 0 and f % 2 == 0:
                        pe.wait_ge(hid_ready, e * PAIRS + f // 2 + 1)
                    ins = pe.matmul(bank(4)[:, d * SL:(d + 1) * SL], w2_s[q][:, f, d * 128:(d + 1) * 128], hid[:, f, :],
                                    start=f == 0, stop=f == KF - 1)
                if d == KD - 1 and KF - 1 in blocks:
                    ins.then_inc(down_done, 1)

            def turn_out(e):
                pe.wait_ge(out_t_ready, e + 1)
                for s in range(SLOT_TILES):
                    for k in range(KD):
                        ins = pe.transpose(bank(6)[0:ST, s * D + k * 128:s * D + (k + 1) * 128],
                                           out_t[:, k, s * ST:(s + 1) * ST], ident)
                ins.then_inc(out_turned, 1)

            def expert(e, q, first=False, last=False):
                up(e, q, 0, not first)
                if not first:
                    turn_out(e - 1)
                up(e, q, 1, not first)
                if not last:
                    look_up(e + 1, 1 - q).then_inc(info_ready, 1)
                for pair in range(2, PAIRS):
                    up(e, q, pair, not first)
                pe.wait_ge(w2_in[q], 8 * (e - q) + 16)
                down(e, q, 0, range(KF))
                down(e, q, 1, range(KF - 2))
                if not last:
                    turn_in(e + 1, 1 - q)
                down(e, q, 1, range(KF - 2, KF))

            drained(pe, "norm2", len(GROUPS) - 1)
            drained(pe, "slots", len(GROUPS) - 1)
            look_up(0, 0, 0, 3).then_inc(info_ready, 1)
            pe.wait_ge(weights_ready, 1)
            look_up(0, 0, 3, b=7).then_inc(weights_looked, 1)
            turn_in(0, 0)
            expert(0, 0, first=True)
            with pe.Fori(0, NE // 2 - 1) as i:
                for j in range(2):
                    expert(2 * i + 1 + j, 1 - j)
            expert(NE - 1, 1, last=True)
            turn_out(NE - 1)


def kernel(x, L0_tok_W, L0_tok_b, L0_tok_cls_token, L0_tok_pos_enc, L0_attn_Wq, L0_attn_Wk, L0_attn_Wo,
           L0_attn_U_b, L0_attn_V_b, L0_attn_W_b, L0_attn_bias_b, L0_attn_U_t, L0_attn_V_t, L0_attn_W_t,
           L0_attn_X_t, L0_attn_bias_t, L0_attn_alpha, L0_ffn_w_router, L0_ffn_b_router, L0_ffn_w1, L0_ffn_b1,
           L0_ffn_w2, L0_ffn_b2):
    import concourse.bacc as bacc
    from concourse.bass_utils import run_bass_kernel_spmd

    def rows(*parts):
        return np.concatenate([np.asarray(p).reshape(-1, D) for p in parts])

    def wide(*parts):
        return np.concatenate([np.asarray(p) for p in parts], 1)

    feats = np.asarray(x).reshape(B, CH, NP_, PATCH, NP_, PATCH).transpose(1, 3, 5, 0, 2, 4).reshape(KP * 128, B, NP2)
    patches = wide(*[blocks(feats[:, a:b].reshape(KP * 128, -1)) for a, b in PATCHES])
    vecs = rows(L0_tok_pos_enc, L0_tok_cls_token, L0_tok_b, L0_attn_bias_b, L0_attn_bias_t)
    vectors = wide(blocks(vecs.T), np.asarray(L0_ffn_b1).reshape(-1, 128).T, np.asarray(L0_ffn_b2).reshape(-1, 128).T,
                   blocks(np.asarray(L0_ffn_w_router)), np.broadcast_to(L0_attn_alpha, (128, 1)),
                   np.broadcast_to(L0_ffn_b_router, (128, NE)))
    attn = wide(blocks(np.asarray(L0_attn_Wq)), blocks(np.asarray(L0_attn_Wk)), blocks(np.asarray(L0_attn_Wo).T),
                blocks(wide(L0_attn_V_b, L0_attn_V_t)), blocks(wide(L0_attn_W_b, L0_attn_W_t)),
                blocks(wide(L0_attn_U_b, L0_attn_U_t)),
                blocks(np.pad(np.asarray(L0_attn_X_t), ((0, 0), (R, 0)))))
    arrays = {"patches": patches, "tok_w": blocks(np.asarray(L0_tok_W).T), "const": constants(), "vectors": vectors,
              "attn": attn, "w1": np.asarray(L0_ffn_w1), "w2": np.asarray(L0_ffn_w2)}
    arrays = {name: np.ascontiguousarray(a) for name, a in arrays.items()}

    nc = bacc.Bacc("TRN2", target_bir_lowering=False, num_devices=1)
    f32 = mybir.dt.float32
    args = [nc.dram_tensor(name, a.shape, f32, kind="ExternalInput").ap() for name, a in arrays.items()]
    args.append(nc.dram_tensor("xrows", (N, D), f32).ap())
    args.append(nc.dram_tensor("out_rows", (N + SL, D), f32, kind="ExternalOutput").ap())
    vit_block(nc, *args)
    got = run_bass_kernel_spmd(nc, [arrays], core_ids=[0]).results[0]["out_rows"]
    return got[:N].reshape(B, T, D)
```

```python
import concourse.bass as bass
from concourse import mybir
from contextlib import ExitStack
import numpy as np

B, CH, IMG, PATCH = 32, 3, 96, 16
NP_ = IMG // PATCH
T = NP_ * NP_ + 1
N = B * T
D = 256
KD = D // 128
R = 64
NE, F = 8, 1024
KF = F // 128
CAP = max(1, int(1.25 * N / NE))
SLOT_TILES = 2
ST = -(-CAP // SLOT_TILES)
PAIRS = KF // 2
SL = ST * SLOT_TILES
TB = 3
TT = TB * T
NT = -(-N // TT)
LAST = N - (NT - 1) * TT
KP = CH * PATCH * PATCH // 128
GROUPS = [(0, 3), (3, 3), (6, 3), (9, 2)]
KEEP_WARM = 3
CHOICES = [(0, 3), (3, 3), (6, 5)]
MADE = [(0, 3), (3, 3), (6, 1), (7, 2), (9, 2)]
PATCHES = [(t0 * TB, min(B, (t0 + n) * TB)) for t0, n in GROUPS]
NP2 = T - 1
FIRST = PATCHES[0][1] * NP2
PIECES = [(0, 1), (1, 3), (3, KP)]
SPLIT = (1, 2)
PARTED = (0,)
GROUP = GROUPS[0][1] * TT
EVEN = GROUP + GROUP % 2
EPS = 1e-5
VECS = T + 4
FLOOR = -87.5
SC = NE * SLOT_TILES
PARTS = 3
NOWHERE = 1000.0


def layout(*widths):
    ends = np.cumsum(widths)
    return [slice(int(e - w), int(e)) for w, e in zip(widths, ends)]


C_ID, C_TRI, C_NEG, C_IOTA, C_IDS, C_TRASH, C_LOW, C_EPS = layout(128, TT, TT, SL + 1, 2 * NT, SC, 1, 1)
A_WQ, A_WK, A_WO, A_V, A_W, A_U, A_X = layout(KD * D, KD * D, KD * D, *(4 * [KD * 2 * R]))
V_VEC, V_B1, V_B2, V_WR, V_ALPHA, V_BR = layout(KD * VECS, NE * KF, NE * KD, KD * NE, 1, NE)


def constants():
    c = np.zeros((128, C_EPS.stop), np.float32)
    c[:, C_ID] = np.eye(128)
    m, n = np.arange(TT)[:, None], np.arange(TT)[None, :]
    c[:TT, C_TRI] = np.where((m // T == n // T) & (m <= n), 1.0 / (n % T + 1), 0.0)
    c[:TT, C_NEG] = np.where(m >= n, -1.0, 0.0)
    c[:, C_IOTA] = np.arange(SL + 1)
    p, t = np.arange(128)[:, None], np.arange(NT)[None, :]
    c[:, C_IDS] = np.stack([p + 1 + 0 * t, 0 * p + t], -1).reshape(128, -1)
    c[:, C_TRASH] = N + p + ST * (np.arange(SC)[None, :] % SLOT_TILES)
    c[:, C_LOW] = np.arange(128)[:, None] < R
    c[:, C_EPS] = EPS
    return c


def blocks(a):
    return a.reshape(-1, 128, a.shape[-1]).transpose(1, 0, 2).reshape(128, -1)


def vit_block(nc, first, patches, const, vectors, attn, w1, w2, xrows, out):
    f32r = mybir.dt.float32r
    f32, bf16, i32, u32 = mybir.dt.float32, mybir.dt.bfloat16, mybir.dt.int32, mybir.dt.uint32
    ALU, ACT, AX = mybir.AluOpType, mybir.ActivationFunctionType, mybir.AxisListType

    with ExitStack() as ctx:
        def sb(name, shape, dt=f32):
            return ctx.enter_context(nc.sbuf_tensor(name, shape, dt))

        def sem(name):
            return ctx.enter_context(nc.semaphore(name))

        cst = sb("cst", [128, C_EPS.stop])
        ident = cst[:, C_ID]
        tri = cst[0:TT, C_TRI]
        iota_slot = cst[0:TT, C_IOTA]
        ids = cst[0:TT, C_IDS]
        trash = cst[0:ST, C_TRASH]
        eps_col = cst[:, C_EPS]
        low_rows = cst[:, C_LOW]

        def wide(ap, k=KD):
            return ap.rearrange("p (k n) -> p k n", k=k)

        def grid(row, tiles, k, n):
            return row.rearrange("p (a b n) -> p a b n", a=1, b=1).broadcast_to((TT, tiles, k, n))

        def spread(per_choice, tiles, n):
            return per_choice.rearrange("p t (k a) -> p t k a", a=1).broadcast_to((TT, tiles, 2, n))

        vecs = sb("vecs", [128, V_BR.stop])
        vec_t = wide(vecs[:, V_VEC])
        b1_t, b2_t = vecs[:, V_B1], vecs[:, V_B2]
        wr_s = wide(vecs[:, V_WR])
        alpha_s = vecs[:, V_ALPHA]
        b_router_s = vecs[0:TT, V_BR]
        att = sb("att", [128, A_X.stop])
        wq_s, wk_s, wo_t, v_cat, w_cat, u_cat, xt_pad = (
            wide(att[:, c]) for c in (A_WQ, A_WK, A_WO, A_V, A_W, A_U, A_X))

        first_t = sb("first_t", [128, KP, D + FIRST])
        tok_wt = first_t[:, :, 0:D]
        patch_t = sb("patch_t", [128, KP * (B * NP2 - FIRST)])
        tok_h, tok_l = (sb(n, [128, KP, D], f32r) for n in ("tok_h", "tok_l"))
        patch_h, patch_l = (sb(n, [128, KP, FIRST], f32r) for n in ("patch_h", "patch_l"))
        h_t = sb("h_t", [128, KD, N])
        h2_t = sb("h2_t", [128, KD, N])
        xn_t, zx_t = (sb(n, [128, KD, GROUP]) for n in ("xn_t", "zx_t"))
        (xn_h, zx_h), (xn_l, zx_l) = (
            [t[:, :, :].rearrange("p k n -> p (k n)")[:, m * KD * EVEN:(m + 1) * KD * EVEN].rearrange(
                "p (k n) -> p k n", k=KD) for m in range(2)] for t in (patch_h, patch_l))
        z_s = sb("z_s", [128, N])
        prod = sb("prod", [128, N])
        xn = sb("xn", [TT, NT, D])
        h2 = sb("h2", [TT, NT, D])
        onehot = sb("onehot", [TT, NT, SL])
        rows_in = [sb(f"rows_in{q}", [ST, SLOT_TILES, D]) for q in range(2)]
        buf_t = [sb(f"buf_t{q}", [128, KD, SL]) for q in range(2)]
        hid = sb("hid", [128, KF, SL])
        out_t = sb("out_t", [128, KD, SL])
        out_s = [sb(f"out_s{q}", [ST, SLOT_TILES, D]) for q in range(2)]
        w1_s = [wide(w, KD) for w in (sb("w1_even", [128, KD * F])[:, :], patch_t[:, 0:KD * F])]
        w2_s = [wide(w, KF) for w in (sb("w2_even", [128, KF * D])[:, :], patch_t[:, KD * F:KD * F + KF * D])]
        m_a = sb("m_a", [128, KD, 2 * R])
        m_c = sb("m_c", [128, KD, 2 * R])
        m_h, m_l = (sb(n, [128, 3, KD, 2 * R], f32r) for n in ("m_h", "m_l"))
        uw = sb("uw", [128, D])
        u_scale = sb("u_scale", [128, 1])
        bias_s = sb("bias_s", [128, KD])
        bias_o = sb("bias_o", [128, KD])
        table = sb("table", [128, KD, T])
        wr_c = sb("wr_c", [128, KD, NE])
        mean_mat = sb("mean_mat", [128, 128])
        ones = sb("ones", [TT, TT], bf16)
        neg_prefix = sb("neg_prefix", [TT, TT], bf16)
        zeros = sb("zeros", [ST, SLOT_TILES * D])
        bn = sb("bn", [TT, 5, 6])
        mv = sb("mv", [TT, 2 * NT, 2])
        rstd = sb("rstd", [TT, 2 * NT])
        std = sb("std", [TT, 2 * NT])
        nmr = sb("nmr", [TT, 2 * NT])
        logit = sb("logit", [TT, NT, NE])
        below = sb("below", [TT, NT, NE + 2])
        floored = sb("floored", [TT, NT, NE])
        largest = sb("largest", [TT, NT])
        top2 = sb("top2", [TT, NT, 8])
        which = sb("which", [TT, NT, 8], u32)
        is_one = sb("is_one", [TT, NT, 2, NE])
        chosen = sb("chosen", [TT, NT, NE], bf16)
        place0 = sb("place0", [TT, NT])
        slot_of = sb("slot_of", [TT, NT, 2])
        by_expert = sb("by_expert", [TT, NT, 2, NE])
        kept = sb("kept", [TT, NT, 2])
        lost = sb("lost", [TT, NT, 2])
        upper = sb("upper", [TT, NT, 2])
        slot_p = sb("slot_p", [TT, NT, 2])
        slot_q = sb("slot_q", [TT, NT, 2])
        at_p = sb("at_p", [TT, NT, 2, ST], bf16)
        at_q = sb("at_q", [TT, NT, 2, SC], bf16)
        id_marks = sb("id_marks", [TT, NT, 2, 2, SC], bf16)
        w_marks = sb("w_marks", [TT, NT, 2, PARTS, SC], bf16)
        expd = sb("expd", [TT, NT, NE + 2])
        weight = sb("weight", [TT, NT, 2])
        parts = sb("parts", [TT, NT, 2, PARTS], bf16)
        every, got = sb("every", [TT, NT]), sb("got", [TT, NT])
        slot_id = sb("slot_id", [ST, SC])
        src_row = sb("src_row", [ST, SC], i32)
        dst_row = sb("dst_row", [ST, SC], i32)
        dst_f = sb("dst_f", [ST, SC])
        src_f = sb("src_f", [ST, SC])
        coef = sb("coef", [ST, SC])
        b1_cur = [sb(f"b1_cur{q}", [128, KF]) for q in range(2)]
        b2_cur = [sb(f"b2_cur{q}", [128, KD]) for q in range(2)]
        coef_cur = [sb(f"coef_cur{q}", [ST, SLOT_TILES]) for q in range(2)]
        idle = sb("idle", [1, 1])

        ps = ctx.enter_context(nc.psum_tensor("ps", [128, 8 * 512], f32))

        def slot(u):
            return ps[:, IN_SLOT[u] * 1024:(IN_SLOT[u] + 1) * 1024]

        def bank(b):
            return ps[:, b * 512:(b + 1) * 512]

        ID_BANK, WEIGHT_BANK = 5, 6
        DOWN_BANKS = (4, 7)
        LAST_BANKS = (6, 5)

        const_in, attn_in, vec_in = sem("const_in"), sem("attn_in"), sem("vec_in")
        first_in = [sem(f"first_in{i}") for i in range(len(PIECES))]
        patch_in = [sem(f"patch_in{g}") for g in range(len(GROUPS))]
        pool_set = sem("pool_set")
        tok_high, tok_split = sem("tok_high"), sem("tok_split")
        patch_high, patch_split = sem("patch_high"), sem("patch_split")
        m_high, zx_high = sem("m_high"), sem("zx_high")
        patch_used = sem("patch_used")
        psum_filled = sem("psum_filled")
        dve_drained = sem("dve_drained")
        act_drained = sem("act_drained")
        dve_step = sem("dve_step")
        var_ready, std_ready = sem("var_ready"), sem("std_ready")
        stats1_ready, stats2_ready = sem("stats1_ready"), sem("stats2_ready")
        rows_stored = [sem(f"rows_stored{g}") for g in range(len(GROUPS))]
        out_stored = sem("out_stored")
        added = sem("added")
        out_free = sem("out_free")
        below_ready, exp_ready = sem("below_ready"), sem("exp_ready")
        coef_ready = sem("coef_ready")
        chosen_ready, weights_ready, weights_looked = sem("chosen_ready"), sem("weights_ready"), sem("weights_looked")
        w1_in = [sem(f"w1_in{q}") for q in range(2)]
        w2_in = [sem(f"w2_in{q}") for q in range(2)]
        onehot_ready, picked = sem("onehot_ready"), sem("picked")
        marks_ready, ids_looked, src_ready, dst_ready = (
            sem(n) for n in ("marks_ready", "ids_looked", "src_ready", "dst_ready"))
        gathered = [sem(f"gathered{q}") for q in range(2)]
        in_turned, buf_ready, half_ready = sem("in_turned"), sem("buf_ready"), sem("half_ready")
        up_done, hid_ready, down_done, out_t_ready = (
            sem(n) for n in ("up_done", "hid_ready", "down_done", "out_t_ready"))
        out_turned, out_s_ready = sem("out_turned"), sem("out_s_ready")
        logits_read, biases_ready = sem("logits_read"), sem("biases_ready")
        slots_known = sem("slots_known")
        prepared = sem("prepared")

        A, B_, C, E = range(len(GROUPS))
        UNITS = [("proj", A, "dve"), ("mac", 0, "act"), ("uw", 0, "dve"), ("proj", B_, "dve"), ("norm1", A, "act"),
                 ("proj", C, "dve"), ("xn_t", A, "dve"), ("zx_t", A, "act"), ("norm1", B_, "act"),
                 ("proj", E, "dve"), ("z", A, "act"), ("ac", A, "dve"), ("xn_t", B_, "dve"), ("zx_t", B_, "act"),
                 ("norm1", C, "act"), ("y", A, "dve"), ("z", B_, "act"), ("ac", B_, "dve"),
                 ("xn_t", C, "dve"), ("zx_t", C, "act"), ("norm1", E, "act"), ("norm2", A, "act"),
                 ("y", B_, "dve"), ("z", C, "act"), ("ac", C, "dve"), ("xn_t", E, "dve"), ("zx_t", E, "act"),
                 ("y", C, "dve"), ("slots", 0, "dve"), ("z", E, "act"), ("ac", E, "dve"), ("norm2", B_, "act"),
                 ("y", E, "dve"), ("norm2", C, "act"), ("norm2", E, "act"), ("slots", 1, "dve"), ("slots", 2, "dve")]
        UNITS = [(kind, n, "dve" if kind == "zx_t" and n in PARTED else reader) for kind, n, reader in UNITS]
        PLACE = {(kind, n): u for u, (kind, n, _) in enumerate(UNITS)}
        IN_SLOT = [u % 4 for u in range(len(UNITS))]
        PICK_SLOT = IN_SLOT[PLACE["z", E]]
        for unit, before in ((("norm2", C), ("ac", E)), (("norm2", E), ("y", E)),
                             (("slots", 1), ("norm2", B_)), (("slots", 2), ("norm2", B_))):
            IN_SLOT[PLACE[unit]] = IN_SLOT[PLACE[before]]

        pick_slot = wide(ps[:, PICK_SLOT * 1024:(PICK_SLOT + 1) * 1024])[:, :, 0:SL]

        def drained(eng, kind, n):
            u = PLACE[kind, n]
            reader = UNITS[u][2]
            eng.wait_ge(act_drained if reader == "act" else dve_drained,
                        sum(1 for v in UNITS[:u + 1] if v[2] == reader))

        def filled(eng, kind, n):
            eng.wait_ge(psum_filled, PLACE[kind, n] + 1)
            return slot(PLACE[kind, n])

        def rows_of(t):
            return TT if t < NT - 1 else LAST

        def patch_cols(g):
            a, b = PATCHES[g]
            return KP * (a * NP2 - FIRST), KP * (b * NP2 - FIRST)

        def tile_parts(a, b):
            return [(TT, a, b)] if b < NT else [(TT, a, NT - 1), (LAST, NT - 1, NT)]

        def group_cols(g):
            t0, n = GROUPS[g]
            return t0 * TT, min(N, (t0 + n) * TT)

        def group_width(g):
            c0, c1 = group_cols(g)
            return c1 - c0

        def raw_patches(g):
            return wide(patch_t[:, slice(*patch_cols(g))], KP)

        block = ctx.enter_context(nc.Block())

        @block.sync
        def _(sp):
            for i, (a, b) in enumerate(PIECES):
                w = D + FIRST
                sp.dma_start(first_t[:, a:b].rearrange("p k d -> p (k d)"), first[:, a * w:b * w]).then_inc(first_in[i], 16)
            sp.dma_start(vecs[:, :], vectors).then_inc(vec_in, 16)
            sp.dma_start(att[:, :], attn).then_inc(attn_in, 16)
            for g in range(1, len(GROUPS)):
                c0, c1 = patch_cols(g)
                sp.dma_start(patch_t[:, c0:c1], patches[:, c0:c1]).then_inc(patch_in[g], 16)
                if g == 1:
                    sp.dma_start(cst[:, :], const).then_inc(const_in, 16)

            def load_w1(e, q):
                sp.dma_start(w1_s[q], w1[e].rearrange("(k p) f -> p k f", p=128)).then_inc(w1_in[q], 16)

            def load_w2(e, q):
                sp.dma_start(w2_s[q], w2[e].rearrange("(k p) d -> p k d", p=128)).then_inc(w2_in[q], 16)

            for e in range(2):
                if e == 1:
                    sp.wait_ge(psum_filled, PLACE["proj", len(GROUPS) - 1] + 1)
                load_w1(e, e)
                load_w2(e, e)
            sp.wait_ge(pool_set, 1)
            sp.dma_start(out[N:N + SL].rearrange("(p s) d -> p (s d)", p=ST), zeros[:, :]).then_inc(out_stored, 16)

            def tile_rows(dram, t0, n):
                return dram[t0 * TT:(t0 + n) * TT].rearrange("(t p) d -> p t d", p=TT)

            for g, (t0, n) in enumerate(GROUPS):
                whole = n - (t0 + n == NT)
                drained(sp, "norm2", g)
                sp.dma_start(tile_rows(xrows, t0, whole), xn[:, t0:t0 + whole]).then_inc(rows_stored[g], 16)
                sp.dma_start(tile_rows(out, t0, whole), h2[:, t0:t0 + whole]).then_inc(out_stored, 16)
                if whole < n:
                    sp.dma_start(xrows[N - LAST:N], xn[0:LAST, NT - 1]).then_inc(rows_stored[g], 16)
                    sp.dma_start(out[N - LAST:N], h2[0:LAST, NT - 1]).then_inc(out_stored, 16)
            with sp.Fori(0, NE // 2 - 1) as i:
                for q in range(2):
                    e = 2 * i + q + 2
                    sp.wait_ge(up_done, (e - 1) * PAIRS)
                    load_w1(e, q)
                    sp.wait_ge(down_done, (e - 1) * KD)
                    load_w2(e, q)

        @block.gpsimd
        def _(pool):
            pool.memset(zeros[:, :], 0.0).then_inc(pool_set, 1)
            pool.memset(mean_mat[:, :], 1.0 / D).then_inc(pool_set, 1)
            pool.memset(u_scale[:, :], 1.0).then_inc(pool_set, 1)
            pool.memset(ones[:, :], 1.0).then_inc(pool_set, 1)
            pool.memset(logit[:, NT - 1:NT], 0.0).then_inc(pool_set, 1)

            def gather(e, q):
                if e > SLOT_TILES:
                    pool.wait_ge(in_turned, e - 2)
                for s in range(SLOT_TILES):
                    c = e * SLOT_TILES + s
                    pool.indirect_dma_start(
                        out=rows_in[q][:, s, :], out_offset=None, in_=xrows[:, :],
                        in_offset=bass.IndirectOffsetOnAxis(ap=src_row[:, c:c + 1], axis=0),
                    ).then_inc(gathered[q], 16)

            def add_out(e, q):
                if e == 0:
                    pool.wait_ge(out_stored, 16 * (len(GROUPS) + 2))
                else:
                    pool.wait_ge(added, e * 16 * SLOT_TILES)
                pool.sem_inc(out_free, 1)
                for s in range(SLOT_TILES):
                    if s == 0 or e == NE - 1:
                        pool.wait_ge(out_s_ready, e + s + 1)
                    c = e * SLOT_TILES + s
                    pool.indirect_dma_start(
                        out=out[:, :], out_offset=bass.IndirectOffsetOnAxis(ap=dst_row[:, c:c + 1], axis=0),
                        in_=out_s[q][:, s, :], in_offset=None, compute_op=ALU.add,
                    ).then_inc(added, 16)

            for g, (t0, n) in enumerate(GROUPS):
                pool.wait_ge(rows_stored[g], 16 * (1 + (t0 + n == NT)))
            pool.wait_ge(src_ready, 1)
            gather(1, 1)
            gather(2, 0)
            pool.wait_ge(dst_ready, 1)
            for e in range(1, NE):
                add_out(e - 1, (e - 1) % 2)
                if e + 2 < NE:
                    gather(e + 2, e % 2)
            add_out(NE - 1, (NE - 1) % 2)
            pool.wait_ge(added, NE * 16 * SLOT_TILES)

        @block.scalar
        def _(act):
            def copy(dst, src):
                return act.activation(dst, src, ACT.Copy)

            stds = [0]

            def take_roots(t0, t1, base):
                stds[0] += 1
                act.wait_ge(var_ready, stds[0])
                for r, a, b in tile_parts(t0, t1):
                    ins = act.activation(std[0:r, base + a:base + b], mv[0:r, base + a:base + b, 1], ACT.Sqrt,
                                         bias=eps_col[0:r])
                ins.then_inc(std_ready, 1)

            def norm1(g):
                take_roots(GROUPS[g][0], sum(GROUPS[g]), 0)
                act.wait_ge(stats1_ready, g + 1)
                p = slot(PLACE["norm1", g])
                t0, n = GROUPS[g]
                for i in range(n):
                    t = t0 + i
                    r = rows_of(t)
                    ins = act.activation(xn[0:r, t], p[0:r, i * D:(i + 1) * D], ACT.Identity,
                                         bias=nmr[0:r, t:t + 1], scale=rstd[0:r, t:t + 1])
                ins.then_inc(act_drained, 1)

            def norm2(g):
                if g < 3:
                    c = CHOICES[g]
                    take_roots(c[0], sum(c), NT)
                    act.wait_ge(stats2_ready, g + 1)
                drained(act, "xn_t", g)
                p = slot(PLACE["norm2", g])
                t0, n = GROUPS[g]
                for i in range(n):
                    t = t0 + i
                    r = rows_of(t)
                    act.activation(xn[0:r, t], p[0:r, i * D:(i + 1) * D], ACT.Identity,
                                   bias=nmr[0:r, NT + t:NT + t + 1], scale=rstd[0:r, NT + t:NT + t + 1])
                whole = n - (t0 + n == NT)
                ins = copy(h2[:, t0:t0 + whole], p[0:TT, 0:whole * D].rearrange("p (t d) -> p t d", t=whole))
                if whole < n:
                    ins = copy(h2[0:LAST, NT - 1], p[0:LAST, whole * D:n * D])
                ins.then_inc(act_drained, 1)

            act.wait_ge(pool_set, 1)
            act.activation(idle[:, :], zeros[0:1, 0:1], ACT.Sqrt)

            for i, (a, b) in enumerate(PIECES):
                act.wait_ge(first_in[i], 16)
                copy(tok_h[:, a:b], tok_wt[:, a:b]).then_inc(tok_high, 1)

            def patches_high(g):
                act.wait_ge(patch_in[g], 16)
                for k in range(KP):
                    if g != SPLIT[0] and k < KP - 1:
                        act.wait_ge(patch_used, (SPLIT.index(g) - 1) * (KP - 1) + k + 1)
                    elif g != SPLIT[0]:
                        act.wait_ge(psum_filled, PLACE["proj", g - 1] + 1)
                    copy(patch_h[:, k], raw_patches(g)[:, k]).then_inc(patch_high, 1)

            patches_high(SPLIT[0])

            for kind, n, reader in UNITS:
                if kind == "zx_t" and n in PARTED:
                    p = filled(act, kind, n).rearrange("p (k s) -> p k s", k=KD)
                    w = group_width(n)
                    copy(zx_h[:, :, 0:w], p[:, :, 0:w]).then_inc(zx_high, 1)
                if reader != "act":
                    continue
                if kind == "mac":
                    p = filled(act, kind, n)
                    copy(m_a[:, :, :], p[:, 0:256].rearrange("p (k r) -> p k r", k=KD))
                    copy(m_c[:, :, :], p[:, 256:512].rearrange("p (k r) -> p k r", k=KD)).then_inc(act_drained, 1)
                    patches_high(SPLIT[1])
                    act.wait_ge(const_in, 16)
                elif kind == "norm1":
                    norm1(n)
                    if n == A:
                        drained(act, "mac", 0)
                        for m, factor in enumerate((m_a, m_c, xt_pad)):
                            copy(m_h[:, m], factor[:, :, :]).then_inc(m_high, 1)
                elif kind == "zx_t":
                    p = filled(act, kind, n).rearrange("p (k s) -> p k s", k=KD)
                    w = group_width(n)
                    copy(zx_t[:, :, 0:w], p[:, :, 0:w]).then_inc(act_drained, 1)
                elif kind == "z":
                    c0, c1 = group_cols(n)
                    p = filled(act, kind, n)
                    act.activation(z_s[:, c0:c1], p[:, 0:c1 - c0], ACT.Identity, bias=low_rows).then_inc(act_drained, 1)
                elif kind == "norm2":
                    norm2(n)
            act.wait_ge(below_ready, 1)
            act.activation(expd[:, :, :], below[:, :, :], ACT.Exp).then_inc(exp_ready, 1)
            act.activation(idle[:, :], eps_col[0:1], ACT.Gelu)

            def hidden(e, q, pair):
                if pair == 0:
                    act.wait_ge(biases_ready, e + 1)
                act.wait_ge(up_done, e * PAIRS + pair + 1)
                for f in (2 * pair, 2 * pair + 1):
                    ins = act.activation(hid[:, f, :], bank(pair)[:, (f % 2) * SL:(f % 2 + 1) * SL], ACT.Gelu,
                                         bias=b1_cur[q][:, f:f + 1])
                ins.then_inc(hid_ready, 1)

            def weigh(e, q):
                act.wait_ge(out_turned, e + 1)
                act.wait_ge(coef_ready, e + 1)
                act.wait_ge(out_free, e + 1)
                for s in range(SLOT_TILES):
                    ins = act.activation(out_s[q][:, s, :], bank(6)[0:ST, s * D:(s + 1) * D], ACT.Copy,
                                         scale=coef_cur[q][:, s:s + 1])
                ins.then_inc(out_s_ready, 1)

            act.wait_ge(picked, 1)
            copy(buf_t[0][:, 1:], pick_slot[:, 1:]).then_inc(half_ready, 1)
            for pair in range(PAIRS):
                hidden(0, 0, pair)
            with act.Fori(0, NE // 2 - 1) as i:
                for j in range(2):
                    e = 2 * i + 1 + j
                    hidden(e, 1 - j, 0)
                    weigh(e - 1, j)
                    for pair in range(1, PAIRS):
                        hidden(e, 1 - j, pair)
            hidden(NE - 1, 1, 0)
            weigh(NE - 2, 0)
            for pair in range(1, PAIRS):
                hidden(NE - 1, 1, pair)
            act.wait_ge(coef_ready, NE)
            act.wait_ge(out_free, NE - 1)
            for s in range(SLOT_TILES):
                act.wait_ge(out_turned, NE + s)
                act.activation(out_s[1][:, s, :], bank(LAST_BANKS[s])[0:ST, 0:D], ACT.Copy,
                               scale=coef_cur[1][:, s:s + 1]).then_inc(out_s_ready, 1)

        @block.vector
        def _(dve):
            steps, stds = [0], [0]

            def step(ins):
                steps[0] += 1
                ins.then_inc(dve_step, 1)
                dve.wait_ge(dve_step, steps[0])

            def read_logits(groups):
                for g in groups:
                    t0, c = GROUPS[g]
                    for r, a, b in tile_parts(t0, t0 + c):
                        raw = slot(PLACE["norm2", g])[0:r, 3 * D + (a - t0) * NE:3 * D + (b - t0) * NE]
                        ins = dve.tensor_tensor(logit[0:r, a:b], raw.rearrange("p (t e) -> p t e", e=NE),
                                                rstd[0:r, NT + a:NT + b].rearrange("p (t a) -> p t a", a=1
                                                                                   ).broadcast_to((r, b - a, NE)), ALU.mult)
                step(ins)
                t0, t1 = GROUPS[groups[0]][0], sum(GROUPS[groups[-1]])
                dve.tensor_tensor(logit[:, t0:t1], logit[:, t0:t1],
                                  b_router_s.rearrange("p (a e) -> p a e", a=1).broadcast_to((TT, t1 - t0, NE)),
                                  ALU.add).then_inc(logits_read, 1)

            def stats(groups, base, ready, read_rest=None, meanwhile=None):
                tiles = [(g, i) for g in groups for i in range(GROUPS[g][1])]
                for b, (g, i) in enumerate(tiles):
                    if i == 0:
                        p = filled(dve, "norm2" if base else "norm1", g)
                    r = rows_of(GROUPS[g][0] + i)
                    ins = dve.bn_stats(bn[0:r, b], p[0:r, i * D:(i + 1) * D])
                step(ins)
                for b, (g, i) in enumerate(tiles):
                    t = GROUPS[g][0] + i
                    ins = dve.bn_aggr(mv[0:rows_of(t), base + t], bn[0:rows_of(t), b])
                ins.then_inc(var_ready, 1)
                stds[0] += 1
                parts = tile_parts(GROUPS[groups[0]][0], sum(GROUPS[groups[-1]]))
                if meanwhile is not None:
                    meanwhile()
                dve.wait_ge(std_ready, stds[0])
                for r, a, b in parts:
                    ins = dve.reciprocal(rstd[0:r, base + a:base + b], std[0:r, base + a:base + b])
                step(ins)
                if read_rest is not None:
                    read_rest(groups)
                for r, a, b in parts:
                    ins = dve.scalar_tensor_tensor(nmr[0:r, base + a:base + b], mv[0:r, base + a:base + b, 0], -1.0,
                                                   rstd[0:r, base + a:base + b], ALU.mult, ALU.mult)
                ins.then_inc(ready, 1)

            dve.wait_ge(vec_in, 16)
            dve.wait_ge(pool_set, 5)
            step(dve.scalar_tensor_tensor(bias_s[:, :], vec_t[:, :, T + 3], alpha_s, vec_t[:, :, T + 2],
                                          ALU.mult, ALU.add))
            for k in range(KD):
                dve.tensor_scalar(table[:, k, 1:T], vec_t[:, k, 1:T], vec_t[:, k, T + 1:T + 2], None, ALU.add)
            dve.tensor_tensor(table[:, :, 0:1], vec_t[:, :, 0:1], vec_t[:, :, T:T + 1], ALU.add)
            step(dve.tensor_copy(u_scale[R:, :], alpha_s[R:, :]))
            step(dve.tensor_copy(h_t[:, :, :].rearrange("p k (b t) -> p k b t", t=T)[:, :, :, 0],
                                 table[:, :, 0:1].broadcast_to((128, KD, B))))
            for i, (a, b) in enumerate(PIECES):
                dve.wait_ge(tok_high, i + 1)
                dve.tensor_tensor(tok_l[:, a:b], tok_wt[:, a:b], tok_h[:, a:b], ALU.subtract).then_inc(tok_split, 1)

            def patches_low(g):
                for k in range(KP):
                    dve.wait_ge(patch_high, SPLIT.index(g) * KP + k + 1)
                    dve.tensor_tensor(patch_l[:, k], raw_patches(g)[:, k], patch_h[:, k], ALU.subtract
                                      ).then_inc(patch_split, 1)

            def set_prefix():
                dve.wait_ge(const_in, 16)
                dve.tensor_copy(neg_prefix[:, :], cst[0:TT, C_NEG]).then_inc(prepared, 1)
            def choose(g):
                t0, n = CHOICES[g]
                tiles = range(t0, t0 + n)
                ts = slice(t0, t0 + n)
                top1 = largest[:, ts].rearrange("p (t a) -> p t a", a=1).broadcast_to((TT, n, NE))
                step(dve.tensor_reduce(largest[:, ts], logit[:, ts], AX.X, ALU.max))
                step(dve.scalar_tensor_tensor(floored[:, ts], top1, FLOOR, logit[:, ts], ALU.add, ALU.max))
                for t in tiles:
                    ins = dve.max(top2[:, t], floored[:, t])
                step(ins)
                for t in tiles:
                    ins = dve.max_index(which[:, t], top2[:, t], floored[:, t])
                step(ins)
                step(dve.tensor_tensor(is_one[:, ts], grid(iota_slot[:, 0:NE], n, 2, NE), spread(which[:, ts, 0:2], n, NE),
                                       ALU.is_equal))
                dve.tensor_tensor(chosen[:, ts], is_one[:, ts, 0], is_one[:, ts, 1], ALU.add).then_inc(chosen_ready, 1)

            def add_up(n):
                c0, c1 = group_cols(n)
                p = filled(dve, "y", n)
                for k in range(KD):
                    ins = dve.scalar_tensor_tensor(h2_t[:, k, c0:c1], p[:, k * 512:k * 512 + c1 - c0], bias_o[:, k:k + 1],
                                                   h_t[:, k, c0:c1], ALU.add, ALU.add)
                ins.then_inc(dve_drained, 1)

            first_slots = iota_slot[:, 1:SL + 1].rearrange("p (a s) -> p a s", a=1)

            def place(g, p):
                t0, n = CHOICES[g]
                ts = slice(t0, t0 + n)
                step(dve.scalar_tensor_tensor(place0[:, ts], p[:, :, 0], 1.0, chosen[:, ts, 0], ALU.add, ALU.mult))
                for a, c in MADE:
                    if t0 <= a < t0 + n:
                        dve.tensor_tensor(onehot[:, a:a + c], first_slots.broadcast_to((TT, c, SL)),
                                          place0[:, a:a + c].rearrange("p (t a) -> p t a", a=1).broadcast_to((TT, c, SL)),
                                          ALU.is_equal).then_inc(onehot_ready, 1)
                dve.tensor_tensor(by_expert[:, ts], is_one[:, ts],
                                  p.rearrange("p t (a e) -> p t a e", a=1).broadcast_to((TT, n, 2, NE)),
                                  ALU.mult).then_inc(dve_drained, 1)

            def know_slots(g):
                drained(dve, "slots", g)
                ts = slice(CHOICES[g][0], sum(CHOICES[g]))
                dve.tensor_reduce(slot_of[:, ts], by_expert[:, ts], AX.X, ALU.add).then_inc(slots_known, 1)
                dve.wait_ge(slots_known, g + 1)

            def place_counts(g):
                c = CHOICES[g][1]
                place(g, filled(dve, "slots", g)[0:TT, 0:c * NE].rearrange("p (t e) -> p t e", e=NE))

            for kind, n, reader in UNITS:
                if (kind, n) == ("proj", SPLIT[0]):
                    patches_low(SPLIT[1])
                if kind == "norm1":
                    stats([n], 0, stats1_ready)
                    if n == A:
                        for m, factor in enumerate((m_a, m_c, xt_pad)):
                            dve.wait_ge(m_high, m + 1)
                            dve.tensor_tensor(m_l[:, m], factor[:, :, :], m_h[:, m], ALU.subtract)
                    continue
                if kind == "norm2":
                    if n < 2:
                        stats([n], NT, stats2_ready, read_logits, (lambda: add_up(E)) if n == 1 else None)
                    elif n == 3:
                        stats([2, 3], NT, stats2_ready, read_logits, lambda: place_counts(1))
                    if n != 2:
                        dve.wait_ge(logits_read, min(n, 2) + 1)
                        choose(min(n, 2))
                    if n == 3:
                        know_slots(1)
                    continue
                if reader != "dve":
                    continue
                if kind == "mac":
                    pass
                elif kind == "uw":
                    set_prefix()
                    patches_low(SPLIT[0])
                    p = filled(dve, kind, n)
                    dve.tensor_scalar(uw[:, :], p[:, 0:D], u_scale[:, 0:1], None, ALU.mult)
                    for k in range(KD):
                        dve.tensor_tensor(wr_c[:, k], wr_s[:, k], p[:, 264:264 + NE], ALU.subtract)
                    dve.tensor_copy(bias_o[:, :], p[:, 256:256 + KD]).then_inc(dve_drained, 1)
                elif kind == "proj":
                    p = filled(dve, kind, n)
                    b0, b1_ = PATCHES[n]
                    nb = b1_ - b0
                    for k in range(KD):
                        dst = h_t[:, k, b0 * T:b1_ * T].rearrange("p (b t) -> p b t", t=T)[:, :, 1:T]
                        src = p[:, k * 512:k * 512 + nb * NP2].rearrange("p (b t) -> p b t", t=NP2)
                        ins = dve.tensor_tensor(dst, src, table[:, k:k + 1, 1:T].broadcast_to((128, nb, NP2)), ALU.add)
                    ins.then_inc(dve_drained, 1)
                elif kind == "xn_t":
                    w = group_width(n)
                    p = filled(dve, kind, n).rearrange("p (k s) -> p k s", k=KD)[:, :, 0:w]
                    if n in PARTED:
                        step(dve.tensor_copy(xn_h[:, :, 0:w], p))
                        dve.tensor_tensor(xn_l[:, :, 0:w], p, xn_h[:, :, 0:w], ALU.subtract).then_inc(dve_drained, 1)
                    else:
                        dve.tensor_copy(xn_t[:, :, 0:w], p).then_inc(dve_drained, 1)
                elif kind == "zx_t":
                    w = group_width(n)
                    p = filled(dve, kind, n).rearrange("p (k s) -> p k s", k=KD)[:, :, 0:w]
                    dve.wait_ge(zx_high, PARTED.index(n) + 1)
                    dve.tensor_tensor(zx_l[:, :, 0:w], p, zx_h[:, :, 0:w], ALU.subtract).then_inc(dve_drained, 1)
                elif kind == "ac":
                    c0, c1 = group_cols(n)
                    p = filled(dve, kind, n)
                    drained(dve, "z", n)
                    step(dve.tensor_tensor(z_s[:, c0:c1], p[:, 512:512 + c1 - c0], z_s[:, c0:c1], ALU.mult))
                    dve.tensor_tensor(prod[:, c0:c1], p[:, 0:c1 - c0], z_s[:, c0:c1], ALU.mult).then_inc(dve_drained, 1)
                elif kind == "y":
                    if n != E:
                        add_up(n)
                elif kind == "slots":
                    if n != 1:
                        place_counts(n)
                        know_slots(n)

            def per_token(c, n):
                return c.rearrange("p (t a) -> p t a", a=1).broadcast_to((TT, NT, n))

            def weigh_tokens():
                dve.wait_ge(exp_ready, 1)
                dve.tensor_reduce(every[:, :], expd[:, :, 0:NE], AX.X, ALU.add)
                step(dve.tensor_tensor(weight[:, :, :], expd[:, :, NE:], kept[:, :, :], ALU.mult))
                step(dve.tensor_reduce(got[:, :], weight[:, :, :], AX.X, ALU.add))
                step(dve.scalar_tensor_tensor(got[:, :], every[:, :], 1e-6, got[:, :], ALU.mult, ALU.max))
                step(dve.reciprocal(got[:, :], got[:, :]))
                step(dve.tensor_tensor(weight[:, :, :], weight[:, :, :], per_token(got[:, :], 2), ALU.mult))
                for c in range(PARTS):
                    step(dve.tensor_copy(parts[:, :, :, c], weight[:, :, :]))
                    if c < PARTS - 1:
                        step(dve.tensor_tensor(weight[:, :, :], weight[:, :, :], parts[:, :, :, c], ALU.subtract))
                for k in range(2):
                    for c in range(PARTS):
                        ins = dve.tensor_tensor(w_marks[:, :, k, c], at_q[:, :, k],
                                                parts[:, :, k, c:c + 1].broadcast_to((TT, NT, SC)), ALU.mult)
                ins.then_inc(weights_ready, 1)

            def read_ids():
                dve.wait_ge(ids_looked, 1)
                row, tile = bank(ID_BANK)[0:ST, 0:SC], bank(ID_BANK)[0:ST, SC:2 * SC]
                step(dve.tensor_copy(slot_id[:, :], row))
                step(dve.scalar_tensor_tensor(slot_id[:, :], tile, float(TT), slot_id[:, :], ALU.mult, ALU.add))
                dve.tensor_scalar(src_row[:, :], slot_id[:, :], -1.0, 0.0, ALU.add, ALU.max).then_inc(src_ready, 1)
                dve.tensor_scalar(src_f[:, :], slot_id[:, :], -1.0, 0.0, ALU.add, ALU.max)
                step(dve.scalar_tensor_tensor(dst_f[:, :], slot_id[:, :], 0.0, trash, ALU.is_equal, ALU.mult))
                step(dve.tensor_tensor(dst_row[:, :], src_f[:, :], dst_f[:, :], ALU.add))

            def read_weights():
                dve.wait_ge(weights_looked, 1)
                part = [bank(WEIGHT_BANK)[0:ST, c * SC:(c + 1) * SC] for c in range(PARTS)]
                step(dve.tensor_copy(coef[:, :], part[0]))
                step(dve.tensor_tensor(coef[:, :], coef[:, :], part[1], ALU.add))
                dve.tensor_tensor(coef[:, :], coef[:, :], part[2], ALU.add).then_inc(dst_ready, 1)
                dve.wait_ge(dst_ready, 1)

            def take_in(e, q, first=False):
                if first:
                    dve.wait_ge(picked, 1)
                    src = pick_slot
                else:
                    dve.wait_ge(in_turned, e)
                    src = wide(bank(5)[:, 0:KD * SL])
                half = slice(0, 1 if first else KD)
                dve.tensor_copy(buf_t[q][:, half], src[:, half]).then_inc(buf_ready, 1)
                dve.tensor_copy(b1_cur[q][:, :], b1_t[:, bass.ds(e * KF, KF)])
                dve.tensor_copy(b2_cur[q][:, :], b2_t[:, bass.ds(e * KD, KD)]).then_inc(biases_ready, 1)

            def read_out(e, q):
                for k in range(KD):
                    dve.wait_ge(down_done, e * KD + k + 1)
                    ins = dve.tensor_scalar(out_t[:, k, :], bank(DOWN_BANKS[k])[:, 0:SL], b2_cur[q][:, k:k + 1],
                                            None, ALU.add)
                ins.then_inc(out_t_ready, 1)

            dve.tensor_tensor(below[:, :, 0:NE], logit[:, :, :], per_token(largest[:, :], NE), ALU.subtract)
            dve.tensor_tensor(below[:, :, NE:], top2[:, :, 0:2], per_token(largest[:, :], 2), ALU.subtract
                              ).then_inc(below_ready, 1)

            dve.tensor_scalar(upper[:, :, :], slot_of[:, :, :], float(ST), None, ALU.is_ge)
            dve.tensor_scalar(kept[:, :, :], slot_of[:, :, :], float(CAP), None, ALU.is_lt)
            step(dve.tensor_scalar(lost[:, :, :], slot_of[:, :, :], float(CAP), NOWHERE, ALU.is_ge, ALU.mult))
            dve.scalar_tensor_tensor(slot_q[:, :, :], which[:, :, 0:2], float(SLOT_TILES), upper[:, :, :], ALU.mult, ALU.add)
            step(dve.scalar_tensor_tensor(slot_p[:, :, :], upper[:, :, :], -float(ST), slot_of[:, :, :], ALU.mult, ALU.add))
            step(dve.tensor_tensor(slot_p[:, :, :], slot_p[:, :, :], lost[:, :, :], ALU.add))
            dve.tensor_tensor(at_q[:, :, :, :], grid(iota_slot[:, 0:SC], NT, 2, SC), spread(slot_q[:, :, :], NT, SC), ALU.is_equal)

            def find_slots(a, b):
                return dve.tensor_tensor(at_p[:, a:b], grid(iota_slot[:, 0:ST], b - a, 2, ST),
                                         spread(slot_p[:, a:b], b - a, ST), ALU.is_equal)

            find_slots(0, 3)
            take_in(0, 0, first=True)
            step(find_slots(3, NT))
            for k in range(2):
                for c in range(2):
                    ins = dve.tensor_tensor(id_marks[:, :, k, c], at_q[:, :, k],
                                            ids.rearrange("p (t c) -> p t c", c=2)[:, :, c:c + 1].broadcast_to((TT, NT, SC)),
                                            ALU.mult)
            ins.then_inc(marks_ready, 1)
            read_ids()
            weigh_tokens()
            read_weights()
            take_in(1, 1)
            for e in range(2):
                dve.tensor_copy(coef_cur[e][:, :], coef[:, e * SLOT_TILES:(e + 1) * SLOT_TILES]).then_inc(coef_ready, 1)
            read_out(0, 0)
            with dve.Fori(0, NE // 2 - 1) as i:
                for j in range(2):
                    e = 2 * i + 1 + j
                    take_in(e + 1, j)
                    dve.wait_ge(out_s_ready, e)
                    dve.tensor_copy(coef_cur[j][:, :], coef[:, bass.ds((e + 1) * SLOT_TILES, SLOT_TILES)]
                                    ).then_inc(coef_ready, 1)
                    read_out(e, 1 - j)
            def last_half(k, cols):
                return dve.tensor_scalar(out_t[:, k, cols], bank(DOWN_BANKS[k])[:, cols], b2_cur[1][:, k:k + 1], None, ALU.add)

            for k in range(KD - 1):
                dve.wait_ge(down_done, (NE - 1) * KD + k + 1)
                last_half(k, slice(0, SL))
            dve.wait_ge(down_done, NE * KD)
            for s in range(SLOT_TILES):
                last_half(KD - 1, slice(s * ST, (s + 1) * ST)).then_inc(out_t_ready, 1)

        @block.tensor
        def _(pe):
            def look_up(marks, dst):
                for t in range(NT):
                    r = rows_of(t)
                    for k in range(2):
                        ins = pe.matmul(dst, at_p[0:r, t, k, :], marks[0:r, t, k].rearrange("p c q -> p (c q)"),
                                        start=t + k == 0, stop=t == NT - 1 and k == 1)
                return ins

            def pick(g):
                if g == 0:
                    drained(pe, "z", E)
                t0, c = CHOICES[g]
                for t in range(t0, t0 + c):
                    for m, (first, _n) in enumerate(GROUPS):
                        if t == first:
                            drained(pe, "norm2", m)
                    for m, (first, _n) in enumerate(MADE):
                        if t == first:
                            pe.wait_ge(onehot_ready, m + 1)
                    r = rows_of(t)
                    for k in range(KD):
                        ins = pe.matmul(pick_slot[:, k, :], xn[0:r, t, k * 128:(k + 1) * 128],
                                        onehot[0:r, t, :], start=t == 0, stop=t == NT - 1)
                return ins

            def keep_warm(products):
                spare = slot(PLACE["slots", 1])[:, 512:640]
                for _ in range(products):
                    pe.matmul(spare, mean_mat[:, :], mean_mat[:, :], start=True, stop=True)

            def factor_product(dst, n, m, factor, src, src_h, src_l):
                products = [(factor, src)]
                if n in PARTED:
                    products = [(m_h[:, m], src_h), (m_l[:, m], src_h), (m_h[:, m], src_l)]
                width = EVEN if n in PARTED else group_width(n)
                for i, (w, x) in enumerate(products):
                    for k in range(KD):
                        ins = pe.matmul(dst[:, 0:width], w[:, k, :], x[:, k, 0:width],
                                        start=i + k == 0, stop=i == len(products) - 1 and k == KD - 1)
                return ins

            def claim(u):
                before = [v for v in range(u) if IN_SLOT[v] == IN_SLOT[u]]
                if before:
                    drained(pe, *UNITS[before[-1]][:2])

            for u, (kind, n, _reader) in enumerate(UNITS):
                claim(u)
                p = slot(u)
                if kind == "mac":
                    pe.wait_ge(attn_in, 16)
                    for m, (w, v) in enumerate(((wq_s, v_cat), (wk_s, w_cat))):
                        for d in range(KD):
                            for k in range(KD):
                                o = m * 256 + d * 128
                                ins = pe.matmul(p[:, o:o + 128], w[:, k, d * 128:(d + 1) * 128], v[:, k, :],
                                                start=k == 0, stop=k == KD - 1)
                elif kind == "uw":
                    pe.wait_ge(dve_step, 1)
                    pe.wait_ge(vec_in, 16)
                    pe.wait_ge(pool_set, 2)
                    for k in range(KD):
                        pe.matmul(p[:, 0:D], u_cat[:, k, :], wo_t[:, k, :], start=k == 0, stop=k == KD - 1)
                    for o in range(KD):
                        for k in range(KD):
                            pe.matmul(p[:, 256 + o:257 + o], wo_t[:, k, o * 128:(o + 1) * 128], bias_s[:, k:k + 1],
                                      start=k == 0, stop=k == KD - 1)
                    for k in range(KD):
                        ins = pe.matmul(p[:, 264:264 + NE], mean_mat[:, :], wr_s[:, k, :], start=k == 0, stop=k == KD - 1)
                elif kind == "proj":
                    nb = PATCHES[n][1] - PATCHES[n][0]
                    if n in SPLIT:
                        pe.wait_ge(tok_split, len(PIECES))
                        products = [(tok_h, patch_h), (tok_l, patch_h), (tok_h, patch_l)]
                        for k in range(KP):
                            pe.wait_ge(patch_split, SPLIT.index(n) * KP + k + 1)
                            for m, (w, x) in enumerate(products):
                                for d in range(KD):
                                    ins = pe.matmul(p[:, d * 512:d * 512 + nb * NP2], w[:, k, d * 128:(d + 1) * 128],
                                                    x[:, k, :], start=k + m == 0, stop=k == KP - 1 and m == 2)
                            if k < KP - 1:
                                ins.then_inc(patch_used, 1)
                        pieces = []
                    elif n == 0:
                        src, pieces = first_t[:, :, D:], PIECES
                    else:
                        src, pieces = wide(patch_t[:, slice(*patch_cols(n))], KP), [(0, KP)]
                        pe.wait_ge(patch_in[n], 16)
                    for i, (a, b) in enumerate(pieces):
                        if n == 0:
                            pe.wait_ge(first_in[i], 16)
                        for d in range(KD):
                            for k in range(a, b):
                                ins = pe.matmul(p[:, d * 512:d * 512 + nb * NP2], tok_wt[:, k, d * 128:(d + 1) * 128],
                                                src[:, k, :], start=k == 0, stop=k == KP - 1)
                elif kind in ("norm1", "norm2"):
                    src = h_t if kind == "norm1" else h2_t
                    if kind == "norm1":
                        pe.wait_ge(const_in, 16)
                        pe.wait_ge(dve_step, 3)
                        drained(pe, "proj", n)
                    else:
                        drained(pe, "y", n)
                    t0, c = GROUPS[n]
                    for i in range(c):
                        r = rows_of(t0 + i)
                        cols = slice((t0 + i) * TT, (t0 + i) * TT + r)
                        for k in range(KD):
                            ins = pe.transpose(p[0:r, i * D + k * 128:i * D + (k + 1) * 128], src[:, k, cols], ident)
                        if kind == "norm2":
                            drained(pe, "uw", 0)
                            for k in range(KD):
                                ins = pe.matmul(p[0:r, 3 * D + i * NE:3 * D + (i + 1) * NE], src[:, k, cols], wr_c[:, k, :],
                                                start=k == 0, stop=k == KD - 1)
                elif kind in ("xn_t", "zx_t"):
                    drained(pe, "norm1", n)
                    t0, c = GROUPS[n]
                    for i in range(c):
                        r = rows_of(t0 + i)
                        for k in range(KD):
                            dst = p[:, k * 512 + i * TT:k * 512 + i * TT + r]
                            src = xn[0:r, t0 + i, k * 128:(k + 1) * 128]
                            if kind == "xn_t":
                                ins = pe.transpose(dst, src, ident[0:r, 0:r])
                            else:
                                ins = pe.matmul(dst, src, tri[0:r, 0:r], start=True, stop=True)
                elif kind == "z":
                    drained(pe, "zx_t", n)
                    ins = factor_product(p[:, 0:512], n, 2, xt_pad, zx_t, zx_h, zx_l)
                elif kind == "ac":
                    drained(pe, "xn_t", n)
                    factor_product(p[:, 0:512], n, 0, m_a, xn_t, xn_h, xn_l)
                    ins = factor_product(p[:, 512:1024], n, 1, m_c, zx_t, zx_h, zx_l)
                elif kind == "y":
                    c0, c1 = group_cols(n)
                    drained(pe, "ac", n)
                    for k in range(KD):
                        ins = pe.matmul(p[:, k * 512:k * 512 + c1 - c0], uw[:, k * 128:(k + 1) * 128], prod[:, c0:c1],
                                        start=True, stop=True)
                elif kind == "slots":
                    pe.wait_ge(prepared, 1)
                    t0, c = CHOICES[n]
                    own = chosen[:, t0:t0 + c].rearrange("p t e -> p (t e)")
                    if n:
                        pe.wait_ge(chosen_ready, n)
                    for t in range(t0):
                        pe.matmul(p[0:TT, 0:c * NE], ones[:, :], chosen[:, t:t + 1].broadcast_to((TT, c, NE)),
                                  start=t == 0, stop=False)
                    pe.wait_ge(chosen_ready, n + 1)
                    pe.matmul(p[0:TT, 0:c * NE], neg_prefix[:, :], own, start=t0 == 0, stop=False)
                    for lag in range(c):
                        ins = pe.matmul(p[0:TT, lag * NE:c * NE], ones[:, :], own[:, 0:(c - lag) * NE],
                                        start=False, stop=lag == c - 1)
                ins.then_inc(psum_filled, 1)
                if (kind, n) == ("norm2", E):
                    pick(0)
                if (kind, n) == ("slots", 1):
                    pick(1)
                if (kind, n) == ("slots", 2):
                    keep_warm(KEEP_WARM)

            def turn_in(e, q):
                pe.wait_ge(gathered[q], 16 * (e + q))
                for k in range(KD):
                    for s in range(SLOT_TILES):
                        ins = pe.transpose(bank(5)[:, k * SL + s * ST:k * SL + (s + 1) * ST],
                                           rows_in[q][:, s, k * 128:(k + 1) * 128], ident[0:ST, 0:ST])
                ins.then_inc(in_turned, 1)

            def up(e, q, pair, reused):
                if pair == 0:
                    pe.wait_ge(w1_in[q], 8 * (e - q) + 16)
                    pe.wait_ge(buf_ready, e + 1)
                if reused:
                    pe.wait_ge(hid_ready, (e - 1) * PAIRS + pair + 1)
                for f in (2 * pair, 2 * pair + 1):
                    for k in range(KD):
                        ins = pe.matmul(bank(pair)[:, (f % 2) * SL:(f % 2 + 1) * SL], w1_s[q][:, k, f * 128:(f + 1) * 128],
                                        buf_t[q][:, k, :], start=k == 0, stop=k == KD - 1)
                ins.then_inc(up_done, 1)

            def down(e, q, d, blocks, reused):
                for f in blocks:
                    if reused and f == 0:
                        pe.wait_ge(out_t_ready, e)
                    if d == 0 and f % 2 == 0:
                        pe.wait_ge(hid_ready, e * PAIRS + f // 2 + 1)
                    ins = pe.matmul(bank(DOWN_BANKS[d])[:, 0:SL], w2_s[q][:, f, d * 128:(d + 1) * 128], hid[:, f, :],
                                    start=f == 0, stop=f == KF - 1)
                ins.then_inc(down_done, 1)

            def turn_out(e):
                pe.wait_ge(out_t_ready, e + 1)
                for s in range(SLOT_TILES):
                    for k in range(KD):
                        ins = pe.transpose(bank(6)[0:ST, s * D + k * 128:s * D + (k + 1) * 128],
                                           out_t[:, k, s * ST:(s + 1) * ST], ident)
                ins.then_inc(out_turned, 1)

            def turn_last(s):
                pe.wait_ge(out_t_ready, NE + s)
                for k in range(KD):
                    ins = pe.transpose(bank(LAST_BANKS[s])[0:ST, k * 128:(k + 1) * 128],
                                       out_t[:, k, s * ST:(s + 1) * ST], ident)
                ins.then_inc(out_turned, 1)

            def expert(e, q, first=False, last=False):
                up(e, q, 0, not first)
                if not first:
                    turn_out(e - 1)
                for pair in range(1, PAIRS):
                    up(e, q, pair, not first)
                    if first and pair == 1:
                        pe.wait_ge(marks_ready, 1)
                        look_up(id_marks, bank(ID_BANK)[0:ST, 0:2 * SC]).then_inc(ids_looked, 1)
                pe.wait_ge(w2_in[q], 8 * (e - q) + 16)
                down(e, q, 0, range(KF), not first)
                if not last:
                    turn_in(e + 1, 1 - q)
                if first:
                    pe.wait_ge(weights_ready, 1)
                    look_up(w_marks, bank(WEIGHT_BANK)[0:ST, 0:PARTS * SC]).then_inc(weights_looked, 1)
                down(e, q, 1, range(KF), not first)
                if last:
                    for s in range(SLOT_TILES):
                        turn_last(s)

            pick(len(CHOICES) - 1).then_inc(picked, 1)
            drained(pe, "norm2", len(GROUPS) - 1)
            drained(pe, "slots", len(CHOICES) - 1)
            pe.wait_ge(half_ready, 1)
            expert(0, 0, first=True)
            with pe.Fori(0, NE // 2 - 1) as i:
                for j in range(2):
                    expert(2 * i + 1 + j, 1 - j)
            expert(NE - 1, 1, last=True)


def kernel(x, L0_tok_W, L0_tok_b, L0_tok_cls_token, L0_tok_pos_enc, L0_attn_Wq, L0_attn_Wk, L0_attn_Wo,
           L0_attn_U_b, L0_attn_V_b, L0_attn_W_b, L0_attn_bias_b, L0_attn_U_t, L0_attn_V_t, L0_attn_W_t,
           L0_attn_X_t, L0_attn_bias_t, L0_attn_alpha, L0_ffn_w_router, L0_ffn_b_router, L0_ffn_w1, L0_ffn_b1,
           L0_ffn_w2, L0_ffn_b2):
    import concourse.bacc as bacc
    from concourse.bass_utils import run_bass_kernel_spmd

    def rows(*parts):
        return np.concatenate([np.asarray(p).reshape(-1, D) for p in parts])

    def wide(*parts):
        return np.concatenate([np.asarray(p) for p in parts], 1)

    feats = np.asarray(x).reshape(B, CH, NP_, PATCH, NP_, PATCH).transpose(1, 3, 5, 0, 2, 4).reshape(KP * 128, B, NP2)
    by_group = [blocks(feats[:, a:b].reshape(KP * 128, -1)) for a, b in PATCHES]
    tok_w = blocks(np.asarray(L0_tok_W).T)
    first = np.concatenate([a.reshape(128, KP, -1) for a in (tok_w, by_group[0])], 2).reshape(128, -1)
    vecs = rows(L0_tok_pos_enc, L0_tok_cls_token, L0_tok_b, L0_attn_bias_b, L0_attn_bias_t)
    vectors = wide(blocks(vecs.T), np.asarray(L0_ffn_b1).reshape(-1, 128).T, np.asarray(L0_ffn_b2).reshape(-1, 128).T,
                   blocks(np.asarray(L0_ffn_w_router)), np.broadcast_to(L0_attn_alpha, (128, 1)),
                   np.broadcast_to(L0_ffn_b_router, (128, NE)))
    attn = wide(blocks(np.asarray(L0_attn_Wq)), blocks(np.asarray(L0_attn_Wk)), blocks(np.asarray(L0_attn_Wo).T),
                blocks(wide(L0_attn_V_b, L0_attn_V_t)), blocks(wide(L0_attn_W_b, L0_attn_W_t)),
                blocks(wide(L0_attn_U_b, L0_attn_U_t)),
                blocks(np.pad(np.asarray(L0_attn_X_t), ((0, 0), (R, 0)))))
    arrays = {"first": first, "patches": wide(*by_group[1:]), "const": constants(), "vectors": vectors,
              "attn": attn, "w1": np.asarray(L0_ffn_w1), "w2": np.asarray(L0_ffn_w2)}
    arrays = {name: np.ascontiguousarray(a) for name, a in arrays.items()}

    nc = bacc.Bacc("TRN2", target_bir_lowering=False, num_devices=1)
    f32 = mybir.dt.float32
    args = [nc.dram_tensor(name, a.shape, f32, kind="ExternalInput").ap() for name, a in arrays.items()]
    args.append(nc.dram_tensor("xrows", (N, D), f32).ap())
    args.append(nc.dram_tensor("out_rows", (N + SL, D), f32, kind="ExternalOutput").ap())
    vit_block(nc, *args)
    got = run_bass_kernel_spmd(nc, [arrays], core_ids=[0]).results[0]["out_rows"]
    return got[:N].reshape(B, T, D)
```
